# Optimizing a Trainium2 kernel written in Bass

```python
import numpy as np
import jax
import jax.numpy as jnp

def _softmax(x, axis=-1):
    return jax.nn.softmax(x, axis=axis)

def _gelu(x):
    return jax.nn.gelu(x, approximate=True)

def _silu(x):
    return jax.nn.silu(x)

def _sigmoid(x):
    return jax.nn.sigmoid(x)

def _layernorm(x, axis=-1, eps=1e-05):
    m = jnp.mean(x, axis=axis, keepdims=True)
    v = jnp.var(x, axis=axis, keepdims=True)
    return (x - m) / jnp.sqrt(v + eps)

def _scatter_add(tgt, idx, src, axis=0):
    return tgt.at[idx].add(src)

def _segment_sum(src, seg, n):
    return jax.ops.segment_sum(src, seg, n)
kernel_name = 'mk_decoder_postln_d1_seqx_r8_f45a67'

def setup_inputs(seed: int=0):
    np.random.seed(seed)
    _w = jnp.asarray

    def _rec_inputs():
        import jax
        import jax.numpy as jnp
        _rk = jax.random.key(seed)
        x = -0.0002928 + 1 * jax.random.normal(jax.random.fold_in(_rk, 1), (64, 64, 128), jnp.float32)
        _lenS = 64 - jax.random.randint(jax.random.fold_in(_rk, 7), (64,), 0, max(1, 64 // 4) + 1, jnp.int32)
        _lenS2 = 64 - jax.random.randint(jax.random.fold_in(_rk, 8), (64,), 0, max(1, 64 // 4) + 1, jnp.int32)
        _ctx_1024P = jax.random.normal(jax.random.fold_in(_rk, 11), (64, 16, 128), jnp.float32)
        _ctx_1024c = jax.random.dirichlet(jax.random.fold_in(_rk, 511), 0.3 * jnp.ones((16,), jnp.float32), (64, 64))
        _ctx_1024t = jnp.einsum('bsk,bkd->bsd', _ctx_1024c, _ctx_1024P)
        _ctx_1024t = _ctx_1024t * jax.lax.rsqrt(jnp.mean(jnp.square(_ctx_1024t)) + 1e-12) * 0.953939
        ctx_1024 = -1.39393e-06 + 0.999914 * (_ctx_1024t + 0.3 * jax.random.normal(jax.random.fold_in(_rk, 611), (64, 64, 128), jnp.float32))
        return (x, ctx_1024)
    x, ctx_1024 = _rec_inputs()

    def _L0_attn_setup():
        import jax, jax.numpy as jnp
        import numpy as np
        H, D, CR, SEL_K = (8, 64, 32, 16)
        ROPE_DIM, THETA, WINDOW, GROUPS = (32, 10000.0, 64, 2)
        INTER, HID, QC = (64, 128, 32)
        NEG = -1e+30

        def _rope_cache(t):
            half = ROPE_DIM // 2
            inv = 1.0 / THETA ** (jnp.arange(half, dtype=jnp.float32) * 2.0 / ROPE_DIM)
            ang = jnp.arange(t, dtype=jnp.float32)[:, None] * inv[None, :]
            return (jnp.cos(ang), jnp.sin(ang))

        def _apply_partial_rope(x, cos, sin):
            half = ROPE_DIM // 2
            x1, x2, rest = (x[..., :half], x[..., half:ROPE_DIM], x[..., ROPE_DIM:])
            return jnp.concatenate([x1 * cos - x2 * sin, x1 * sin + x2 * cos, rest], -1)

        def _rmsnorm(x, g, eps=1e-06):
            return x * jax.lax.rsqrt(jnp.mean(x * x, -1, keepdims=True) + eps) * g
        key = jax.random.key(seed)
        ks = jax.random.split(key, 9)
        f = lambda k, shp, s: jax.random.normal(k, shp, jnp.float32) * s
        return {'h': f(ks[0], (1, 256, HID), 1.0), 'w_qc': f(ks[1], (HID, QC), QC ** (-0.5)), 'w_qup': f(ks[2], (QC, H * D), (H * D) ** (-0.5)), 'w_k': f(ks[3], (HID, D), HID ** (-0.5)), 'w_v': f(ks[4], (HID, D), HID ** (-0.5)), 'g_qnorm': jnp.ones((D,), jnp.float32), 'g_knorm': jnp.ones((D,), jnp.float32), 'w_gate': f(ks[5], (D, 3), 0.05), 'b_gate': jnp.zeros((3,), jnp.float32), 'sink_logit': f(ks[6], (H,), 0.1), 'w_out_group': f(ks[7], (GROUPS, H // GROUPS * D, INTER), 0.05), 'w_out': f(ks[8], (GROUPS * INTER, HID), 0.03)}
    _L0_attn_all = _L0_attn_setup()
    _L0_attn_in = {k: v for k, v in _L0_attn_all.items() if k in ('w_qc', 'w_qup', 'w_k', 'w_v', 'g_qnorm', 'g_knorm', 'w_gate', 'b_gate', 'sink_logit', 'w_out_group', 'w_out')}
    del _L0_attn_all

    def _L0_xattn_setup():
        import jax, jax.numpy as jnp
        import numpy as np
        H = 16
        D_MODEL = 128
        D_K = D_MODEL // H

        def _split_heads(x, B, S):
            return x.reshape(B, S, H, D_K).transpose(0, 2, 1, 3)
        key = jax.random.key(seed)
        ks = jax.random.split(key, 11)
        B, S, D = (2, 256, D_MODEL)
        sc = 1.0 / np.sqrt(D)
        return {'query': jax.random.normal(ks[0], (B, S, D), jnp.float32), 'key': jax.random.normal(ks[1], (B, S, D), jnp.float32), 'value': jax.random.normal(ks[2], (B, S, D), jnp.float32), 'Wq': jax.random.normal(ks[3], (D, D), jnp.float32) * sc, 'bq': jnp.zeros((D,), jnp.float32), 'Wk': jax.random.normal(ks[4], (D, D), jnp.float32) * sc, 'bk': jnp.zeros((D,), jnp.float32), 'Wv': jax.random.normal(ks[5], (D, D), jnp.float32) * sc, 'bv': jnp.zeros((D,), jnp.float32), 'Wo': jax.random.normal(ks[6], (D, D), jnp.float32) * sc, 'bo': jnp.zeros((D,), jnp.float32)}
    _L0_xattn_all = _L0_xattn_setup()
    _L0_xattn_in = {k: v for k, v in _L0_xattn_all.items() if k in ('Wq', 'bq', 'Wk', 'bk', 'Wv', 'bv', 'Wo', 'bo')}
    del _L0_xattn_all

    def _L0_ffn_setup():
        import jax, jax.numpy as jnp
        import numpy as np
        B, S, D = (1, 256, 128)
        I = 256
        E = 8
        K = 2
        LIMIT = 7.0
        ALPHA = 1.702
        EPS = 1e-05

        def _swiglu(h):
            x_glu = jnp.minimum(h[..., ::2], LIMIT)
            x_lin = jnp.clip(h[..., 1::2], -LIMIT, LIMIT)
            return x_glu * jax.nn.sigmoid(ALPHA * x_glu) * (x_lin + 1.0)

        def _moe(t, gate_w, gate_b, mlp1_w, mlp1_b, mlp2_w, mlp2_b):
            T = t.shape[0]
            logits = t @ gate_w + gate_b
            top_v, top_i = jax.lax.top_k(logits, K)
            probs = jax.nn.softmax(top_v, axis=-1)
            w = jnp.zeros((T, E), t.dtype).at[jnp.arange(T)[:, None], top_i].set(probs)

            def body(acc, ew):
                w1, b1, w2, b2, we = ew
                h = _swiglu(t @ w1 + b1)
                y = h @ w2 + b2
                return (acc + we[:, None] * y, None)
            acc0 = jnp.zeros((T, t.shape[1]), t.dtype)
            acc, _ = jax.lax.scan(body, acc0, (mlp1_w, mlp1_b, mlp2_w, mlp2_b, w.T))
            return acc
        key = jax.random.key(seed)
        ks = jax.random.split(key, 4)
        s = 0.02
        return {'x': jax.random.normal(ks[0], (B, S, D), jnp.float32), 'norm_scale': jnp.ones((D,), jnp.float32), 'gate_w': jax.random.normal(ks[1], (D, E), jnp.float32) * s, 'gate_b': jnp.zeros((E,), jnp.float32), 'mlp1_w': jax.random.normal(ks[2], (E, D, 2 * I), jnp.float32) * s, 'mlp1_b': jnp.zeros((E, 2 * I), jnp.float32), 'mlp2_w': jax.random.normal(ks[3], (E, I, D), jnp.float32) * s, 'mlp2_b': jnp.zeros((E, D), jnp.float32)}
    _L0_ffn_all = _L0_ffn_setup()
    _L0_ffn_in = {k: v for k, v in _L0_ffn_all.items() if k in ('norm_scale', 'gate_w', 'gate_b', 'mlp1_w', 'mlp1_b', 'mlp2_w', 'mlp2_b')}
    del _L0_ffn_all
    return {'x': x, 'ctx_1024': ctx_1024, 'L0_attn_w_qc': _L0_attn_in['w_qc'], 'L0_attn_w_qup': _L0_attn_in['w_qup'], 'L0_attn_w_k': _L0_attn_in['w_k'], 'L0_attn_w_v': _L0_attn_in['w_v'], 'L0_attn_g_qnorm': _L0_attn_in['g_qnorm'], 'L0_attn_g_knorm': _L0_attn_in['g_knorm'], 'L0_attn_w_gate': _L0_attn_in['w_gate'], 'L0_attn_b_gate': _L0_attn_in['b_gate'], 'L0_attn_sink_logit': _L0_attn_in['sink_logit'], 'L0_attn_w_out_group': _L0_attn_in['w_out_group'], 'L0_attn_w_out': _L0_attn_in['w_out'], 'L0_xattn_Wq': _L0_xattn_in['Wq'], 'L0_xattn_bq': _L0_xattn_in['bq'], 'L0_xattn_Wk': _L0_xattn_in['Wk'], 'L0_xattn_bk': _L0_xattn_in['bk'], 'L0_xattn_Wv': _L0_xattn_in['Wv'], 'L0_xattn_bv': _L0_xattn_in['bv'], 'L0_xattn_Wo': _L0_xattn_in['Wo'], 'L0_xattn_bo': _L0_xattn_in['bo'], 'L0_ffn_norm_scale': _L0_ffn_in['norm_scale'], 'L0_ffn_gate_w': _L0_ffn_in['gate_w'], 'L0_ffn_gate_b': _L0_ffn_in['gate_b'], 'L0_ffn_mlp1_w': _L0_ffn_in['mlp1_w'], 'L0_ffn_mlp1_b': _L0_ffn_in['mlp1_b'], 'L0_ffn_mlp2_w': _L0_ffn_in['mlp2_w'], 'L0_ffn_mlp2_b': _L0_ffn_in['mlp2_b']}

def reference(x, ctx_1024, L0_attn_w_qc, L0_attn_w_qup, L0_attn_w_k, L0_attn_w_v, L0_attn_g_qnorm, L0_attn_g_knorm, L0_attn_w_gate, L0_attn_b_gate, L0_attn_sink_logit, L0_attn_w_out_group, L0_attn_w_out, L0_xattn_Wq, L0_xattn_bq, L0_xattn_Wk, L0_xattn_bk, L0_xattn_Wv, L0_xattn_bv, L0_xattn_Wo, L0_xattn_bo, L0_ffn_norm_scale, L0_ffn_gate_w, L0_ffn_gate_b, L0_ffn_mlp1_w, L0_ffn_mlp1_b, L0_ffn_mlp2_w, L0_ffn_mlp2_b):
    import jax
    import jax.numpy as jnp

    def _L0_attn_ref(h, w_qc, w_qup, w_k, w_v, g_qnorm, g_knorm, w_gate, b_gate, sink_logit, w_out_group, w_out):
        import jax, jax.numpy as jnp
        import numpy as np
        H, D, CR, SEL_K = (8, 64, 32, 16)
        ROPE_DIM, THETA, WINDOW, GROUPS = (32, 10000.0, 64, 2)
        INTER, HID, QC = (64, 128, 32)
        NEG = -1e+30

        def _rope_cache(t):
            half = ROPE_DIM // 2
            inv = 1.0 / THETA ** (jnp.arange(half, dtype=jnp.float32) * 2.0 / ROPE_DIM)
            ang = jnp.arange(t, dtype=jnp.float32)[:, None] * inv[None, :]
            return (jnp.cos(ang), jnp.sin(ang))

        def _apply_partial_rope(x, cos, sin):
            half = ROPE_DIM // 2
            x1, x2, rest = (x[..., :half], x[..., half:ROPE_DIM], x[..., ROPE_DIM:])
            return jnp.concatenate([x1 * cos - x2 * sin, x1 * sin + x2 * cos, rest], -1)

        def _rmsnorm(x, g, eps=1e-06):
            return x * jax.lax.rsqrt(jnp.mean(x * x, -1, keepdims=True) + eps) * g
        b, t, _ = h.shape
        cos, sin = _rope_cache(t)
        q = (h @ w_qc @ w_qup).reshape(b, t, H, D).transpose(0, 2, 1, 3)
        q = _rmsnorm(_apply_partial_rope(q, cos, sin), g_qnorm)
        k = _rmsnorm(_apply_partial_rope(h @ w_k, cos, sin), g_knorm)
        v = h @ w_v
        scale = 1.0 / np.sqrt(D).astype(np.float32)
        qpos = jnp.arange(t)
        sink = jnp.broadcast_to(sink_logit[None, :, None, None], (b, H, t, 1))
        nb = t // CR
        kc = k[:, :nb * CR].reshape(b, nb, CR, D).mean(2)
        vc = v[:, :nb * CR].reshape(b, nb, CR, D).mean(2)
        comp_valid = ((jnp.arange(nb) + 1) * CR - 1)[None, :] <= qpos[:, None]
        any_blk = comp_valid.any(-1, keepdims=True)
        safe = jnp.where(any_blk, comp_valid, True)
        sc_raw = jnp.einsum('bhqd,bnd->bhqn', q, kc) * scale
        pc = jax.nn.softmax(jnp.concatenate([jnp.where(safe, sc_raw, NEG), sink], -1), -1)
        comp_out = jnp.einsum('bhqn,bnd->bhqd', pc[..., :nb], vc)
        comp_out = jnp.where(any_blk[None, None], comp_out, 0.0)
        sel_sc = jnp.where(comp_valid, sc_raw, -jnp.inf)
        top_idx = jax.lax.top_k(sel_sc, min(SEL_K, nb))[1]
        sel_blocks = (top_idx[..., :, None] == jnp.arange(nb)).any(-2)
        block_of = jnp.minimum(qpos // CR, nb - 1)
        causal = qpos[:, None] >= qpos[None, :]
        in_range = qpos < nb * CR
        tok_sel = sel_blocks[..., block_of] & (causal & in_range[None, :])[None, None]
        scores_full = jnp.einsum('bhqd,bkd->bhqk', q, k) * scale
        ps = jax.nn.softmax(jnp.where(tok_sel, scores_full, NEG), -1)
        sel_out = jnp.einsum('bhqk,bkd->bhqd', ps, v)
        sw = causal & (qpos[:, None] - qpos[None, :] < WINDOW)
        pw = jax.nn.softmax(jnp.concatenate([jnp.where(sw[None, None], scores_full, NEG), sink], -1), -1)
        sw_out = jnp.einsum('bhqk,bkd->bhqd', pw[..., :t], v)
        g = jax.nn.sigmoid(q @ w_gate + b_gate)
        g = g / jnp.clip(g.sum(-1, keepdims=True), 1e-06)
        mixed = g[..., 0:1] * comp_out + g[..., 1:2] * sel_out + g[..., 2:3] * sw_out
        x = mixed.transpose(0, 2, 1, 3).reshape(b, t, GROUPS, H // GROUPS * D)
        y = jnp.einsum('btgf,gfi->btgi', x, w_out_group).reshape(b, t, GROUPS * INTER)
        return y @ w_out

    def _L0_xattn_ref(query, key, value, Wq, bq, Wk, bk, Wv, bv, Wo, bo):
        import jax, jax.numpy as jnp
        import numpy as np
        H = 16
        D_MODEL = 128
        D_K = D_MODEL // H

        def _split_heads(x, B, S):
            return x.reshape(B, S, H, D_K).transpose(0, 2, 1, 3)
        B, S, D = query.shape
        q = _split_heads(query @ Wq + bq, B, S)
        k = _split_heads(key @ Wk + bk, B, key.shape[1])
        v = _split_heads(value @ Wv + bv, B, value.shape[1])
        scores = jnp.einsum('bhqd,bhkd->bhqk', q, k) / jnp.sqrt(jnp.asarray(D_K, q.dtype))
        p_attn = jax.nn.softmax(scores, axis=-1)
        x = jnp.einsum('bhqk,bhkd->bhqd', p_attn, v)
        x = x.transpose(0, 2, 1, 3).reshape(B, S, H * D_K)
        return x @ Wo + bo

    def _L0_ffn_ref(x, norm_scale, gate_w, gate_b, mlp1_w, mlp1_b, mlp2_w, mlp2_b):
        import jax, jax.numpy as jnp
        import numpy as np
        B, S, D = (1, 256, 128)
        I = 256
        E = 8
        K = 2
        LIMIT = 7.0
        ALPHA = 1.702
        EPS = 1e-05

        def _swiglu(h):
            x_glu = jnp.minimum(h[..., ::2], LIMIT)
            x_lin = jnp.clip(h[..., 1::2], -LIMIT, LIMIT)
            return x_glu * jax.nn.sigmoid(ALPHA * x_glu) * (x_lin + 1.0)

        def _moe(t, gate_w, gate_b, mlp1_w, mlp1_b, mlp2_w, mlp2_b):
            T = t.shape[0]
            logits = t @ gate_w + gate_b
            top_v, top_i = jax.lax.top_k(logits, K)
            probs = jax.nn.softmax(top_v, axis=-1)
            w = jnp.zeros((T, E), t.dtype).at[jnp.arange(T)[:, None], top_i].set(probs)

            def body(acc, ew):
                w1, b1, w2, b2, we = ew
                h = _swiglu(t @ w1 + b1)
                y = h @ w2 + b2
                return (acc + we[:, None] * y, None)
            acc0 = jnp.zeros((T, t.shape[1]), t.dtype)
            acc, _ = jax.lax.scan(body, acc0, (mlp1_w, mlp1_b, mlp2_w, mlp2_b, w.T))
            return acc
        Bx, Sx, Dx = x.shape
        ms = jnp.mean(x * x, axis=-1, keepdims=True)
        t = (x * jax.lax.rsqrt(ms + EPS) * norm_scale).reshape(Bx * Sx, Dx)
        y = _moe(t, gate_w, gate_b, mlp1_w, mlp1_b, mlp2_w, mlp2_b)
        return x + y.reshape(Bx, Sx, Dx)
    x = _layernorm(x + _L0_attn_ref(x, L0_attn_w_qc, L0_attn_w_qup, L0_attn_w_k, L0_attn_w_v, L0_attn_g_qnorm, L0_attn_g_knorm, L0_attn_w_gate, L0_attn_b_gate, L0_attn_sink_logit, L0_attn_w_out_group, L0_attn_w_out), axis=-1)
    x = _layernorm(x + _L0_xattn_ref(x, ctx_1024, ctx_1024, L0_xattn_Wq, L0_xattn_bq, L0_xattn_Wk, L0_xattn_bk, L0_xattn_Wv, L0_xattn_bv, L0_xattn_Wo, L0_xattn_bo), axis=-1)
    x = _layernorm(x + _L0_ffn_ref(x, L0_ffn_norm_scale, L0_ffn_gate_w, L0_ffn_gate_b, L0_ffn_mlp1_w, L0_ffn_mlp1_b, L0_ffn_mlp2_w, L0_ffn_mlp2_b), axis=-1)
    return x

_drawn_inputs = setup_inputs


def setup_inputs(seed=0):
    import zlib

    import numpy as np

    out = dict(_drawn_inputs(seed))
    spreads = {'L0_attn_g_qnorm': (1.0, 0.6),
     'L0_attn_g_knorm': (1.0, 0.6),
     'L0_attn_b_gate': (0.0, 2.0),
     'L0_xattn_bq': (0.0, 0.32),
     'L0_xattn_bk': (0.0, 2.0),
     'L0_xattn_bv': (0.0, 0.1),
     'L0_xattn_bo': (0.0, 0.1),
     'L0_ffn_norm_scale': (1.0, 0.6),
     'L0_ffn_gate_b': (0.0, 0.281),
     'L0_ffn_mlp1_b': (0.0, 0.8),
     'L0_ffn_mlp2_b': (0.0, 0.272)}
    factors = {'L0_attn_w_gate': 8.0,
     'L0_attn_sink_logit': 8.0,
     'L0_ffn_mlp1_w': 4.006,
     'L0_ffn_mlp2_w': 3.597}
    for name, (base, spread) in spreads.items():
        noise = np.random.default_rng([zlib.crc32(name.encode()), seed]).standard_normal(out[name].shape)
        drawn = base * np.exp(spread * noise) if base else spread * noise
        out[name] = jnp.asarray(drawn.astype(out[name].dtype))
    for name, factor in factors.items():
        out[name] = (out[name] * factor).astype(out[name].dtype)
    return out
```

```python
import numpy as np
import concourse.bass as bass
from concourse import mybir
from concourse.alu_op_type import AluOpType as ALU
from contextlib import ExitStack

F32 = mybir.dt.float32
BF16 = mybir.dt.bfloat16
ACT = mybir.ActivationFunctionType
AX = mybir.AxisListType
P = 128
T = 64
NEG = -1.0e30


class Count:

    def __init__(self, eng, sem):
        self.eng, self.sem, self.n, self.shift = eng, sem, 0, None

    def add(self, ins):
        self.n += 1
        ins.then_inc(self.sem, 1)
        return self.n

    def upto(self, n):
        self.eng.wait_ge(self.sem, n if self.shift is None else self.shift + n)

    def settle(self):
        self.upto(self.n)


class Tile:

    def __init__(self, at, lag):
        i, u, unroll, tiles = at
        self.i, self.c, self.unroll = i, u - lag, unroll
        self.static = isinstance(i, int)
        self.t = i * unroll + self.c
        self.live = not self.static or 0 <= self.t < tiles
        self.u2, self.u4 = self.c % 2, self.c % 4

    def wait(self, eng, sem, per=1):
        eng.wait_ge(sem, (self.t + 1) * per)

    def free(self, eng, sem, ahead, per=1):
        if not self.static or self.t >= ahead:
            eng.wait_ge(sem, (self.t + 1 - ahead) * per)

    def ring(self, sems, back=0):
        return sems[(self.c - back) % len(sems)]

    def wait_ring(self, eng, sems, per, back=0):
        if not self.static or self.t >= back:
            n = len(sems)
            eng.wait_ge(self.ring(sems, back), (self.i * (self.unroll // n) + (self.c - back) // n + 1) * per)


def carry(eng, passed):
    eng.sem_inc(passed, 1)


def pipeline(eng, slot, tiles, lags, unroll, counts=()):
    first = -(-(lags + 2) // unroll)
    for s in range(first * unroll):
        before = [c.n for c in counts]
        slot((s // unroll, s % unroll, unroll, tiles))
    per = [unroll * (c.n - b) for c, b in zip(counts, before)]
    rounds = tiles // unroll
    assert tiles % unroll == 0 and rounds > first
    start = [c.n for c in counts]
    with eng.Fori(first, rounds) as i:
        for c, p in zip(counts, per):
            c.shift = (i - first) * p
        for u in range(unroll):
            slot((i, u, unroll, tiles))
    for c, p, b in zip(counts, per, start):
        assert c.n - b == p, (c.n - b, p)
        c.n, c.shift = b + p * (rounds - first), None
    for s in range(tiles, tiles + lags):
        slot((s // unroll, s % unroll, unroll, tiles))


def attention(nc, x, xT, w_qcT, w_qup, w_k, w_v, g_q, g_k, w_gate, b_gate, sink, w_ogT, w_out,
              rope_cos, rope_sin, mask, ident, v_dram, x1, tiles):
    H, D, W = 8, 64, 69
    GW = 4 * W
    LAG, U = 9, 4
    with ExitStack() as ctx:
        def sb(name, shape, dt=F32):
            return ctx.enter_context(nc.sbuf_tensor("a_" + name, shape, dt))

        def sem(name):
            return ctx.enter_context(nc.semaphore("a_" + name))

        wqcT = sb("wqcT", [32, P])
        wqup = sb("wqup", [32, H * D])
        wqkv = sb("wqkv", [P, H * D + 2 * D])
        wogT = sb("wogT", [D, 2, 256])
        wout = sb("wout", [D, 2, P])
        wc = sb("wc", [P, 4, P])
        gq = sb("gq", [P, D])
        gk = sb("gk", [P, D])
        gg = sb("gg", [P, 2, D])
        gqc = sb("gqc", [P, 1])
        wgate = sb("wgate", [P, 3])
        wg = sb("wg", [P, 3])
        bg = sb("bg", [P, 3])
        snk = sb("snk", [P, H])
        cos = sb("cos", [P, 32])
        sin = sb("sin", [P, 32])
        maskf = sb("maskf", [P, GW])
        maskb = sb("maskb", [P, GW], BF16)
        idf = sb("idf", [P, P])
        idb = sb("idb", [P, P], BF16)
        halfneg = sb("halfneg", [P, 16])
        root = sb("root", [P, H])
        xTt = sb("xTt", [P, 2, P])
        xt = sb("xt", [P, 2, P])
        qk = sb("qk", [P, 4, 9, D])
        sq = sb("sq", [P, 2, 9, D])
        ta = sb("ta", [P, 9, 32])
        tb = sb("tb", [P, 9, 32])
        ss = sb("ss", [P, 9])
        ms = sb("ms", [P, 2, 9])
        rinv = sb("rinv", [P, 4, 9])
        kd = sb("kd", [P, 2, 2, D])
        vs = sb("vs", [P, 2, D])
        VB = sb("VB", [P, 4, 2, P])
        qT = sb("qT", [P, 2, 4, P])
        KB = sb("KB", [P, 2, 2, 2, W])
        mx = sb("mx", [P, H])
        s5 = sb("s5", [P, 2, H, 5])
        sc8 = sb("sc8", [P, 4, H])
        gl = sb("gl", [P, H, 3])
        nbg = sb("nbg", [P, 3])
        Z = sb("Z", [P, 2, H])
        a3 = sb("a3", [P, H])
        nb = sb("nb", [P, 2, H])
        un = sb("un", [P, H, 2])
        mc = sb("mc", [P, H])
        arg = sb("arg", [P, 2, H, 7])
        ex = sb("ex", [P, 2, H, 7])
        den = sb("den", [P, H, 6])
        rd = sb("rd", [P, H, 6])
        gs = sb("gs", [P, H])
        rg = sb("rg", [P, H])
        a1 = sb("a1", [P, H])
        a2 = sb("a2", [P, H])
        pa = sb("pa", [P, 2, H])
        pc = sb("pc", [P, 2, H, 2])
        E = sb("E", [P, 4, H, D])
        Pm = sb("Pm", [P, 2, H, D])
        PT = sb("PT", [P, 4, P])
        mT = sb("mT", [P, 4, P])
        r = sb("r", [P, 2, P])
        st = sb("st", [P, 6])
        mv = sb("mv", [P, 2, 2])
        ve = sb("ve", [P, 2, 1])
        rs = sb("rs", [P, 2, 1])
        xo = sb("xo", [P, 2, P])

        ps = ctx.enter_context(nc.psum_tensor("a_ps", [P, 8, 512], F32))
        flat = ps[:, 0:2, :].rearrange("p a b -> p (a b)")
        ps_qk = flat[:, 0:9 * D].rearrange("p (h d) -> p h d", d=D)
        ps_v = flat[:, 9 * D:10 * D]
        ps_y = ps[:, 1, 256:256 + P]
        ps_qT, ps_kT = ps[:, 2, :], ps[:, 3, 0:P]
        ps_S = ps[:, 4:6, 0:GW]
        ps_Sh = ps_S.rearrange("p a (h w) -> p a h w", w=W)
        ps_PT, ps_mT = ps[:, 6, :], ps[:, 7, :]

        loaded = sem("loaded")
        made = sem("made")
        prods = sem("prods")
        weights = sem("weights")
        xT_in, x_in, stored = ([sem(f"{k}{i}") for i in range(2)] for k in ("xT_in", "x_in", "stored"))
        v_spread, v_kept = ([sem(f"{k}{i}") for i in range(4)] for k in ("v_spread", "v_kept"))
        sined, scores_kept, gate_args, scales = sem("sined"), sem("scores_kept"), sem("gate_args"), sem("scales")
        projected, kq_copied, squared, v_copied = sem("projected"), sem("kq_copied"), sem("squared"), sem("v_copied")
        roped, mean_sq, inv_rms, k_normed = sem("roped"), sem("mean_sq"), sem("inv_rms"), sem("k_normed")
        turned, qT_copied, kT_copied, k_means = sem("turned"), sem("qT_copied"), sem("kT_copied"), sem("k_means")
        scored, maxed, exped, args, small_exp = sem("scored"), sem("maxed"), sem("exped"), sem("args"), sem("small_exp")
        mixing, mixed, P_turned, PT_copied = sem("mixing"), sem("mixed"), sem("P_turned"), sem("PT_copied")
        summed, mT_copied, y_done, y_added = sem("summed"), sem("mT_copied"), sem("y_done"), sem("y_added")
        ln_var, ln_rstd, x1_done = sem("ln_var"), sem("ln_rstd"), sem("x1_done")
        dve_n, act_n, pool_n = sem("dve_n"), sem("act_n"), sem("pool_n")
        sp_passed, dve_passed = sem("sp_passed"), sem("dve_passed")
        NLOAD = 18

        block = ctx.enter_context(nc.Block())

        @block.sync
        def _(sp):
            loads = [
                (wqcT[:, :], w_qcT), (wqup[:, :], w_qup),
                (wqkv[:, H * D:H * D + D], w_k), (wqkv[:, H * D + D:], w_v),
                (wogT[:, :, :], w_ogT.rearrange("g i f -> i g f")),
                (wout[:, :, :], w_out.rearrange("(g i) n -> i g n", g=2)),
                (gq[:, :], g_q.partition_broadcast(P)), (gk[:, :], g_k.partition_broadcast(P)),
                (gqc[0:D, :], g_q.rearrange("(d a) -> d a", a=1)), (gqc[D:P, :], g_q.rearrange("(d a) -> d a", a=1)),
                (wgate[0:D, :], w_gate), (wgate[D:P, :], w_gate),
                (bg[:, :], b_gate.partition_broadcast(P)), (snk[:, :], sink.partition_broadcast(P)),
                (cos[:, :], rope_cos), (sin[:, :], rope_sin), (maskf[:, :], mask), (idf[:, :], ident),
            ]
            assert len(loads) == NLOAD
            for dst, src in loads:
                sp.dma_start(dst, src).then_inc(loaded, 16)

            def slot(at):
                a = Tile(at, 0)
                if a.live:
                    a.free(sp, projected, 2)
                    carry(sp, sp_passed)
                    sp.dma_start(xTt[:, a.u2, :], xT[:, bass.ds(a.t * P, P)]).then_inc(a.ring(xT_in), 16)
                b = Tile(at, 1)
                if b.live:
                    b.wait(sp, v_copied)
                    carry(sp, sp_passed)
                    sp.dma_start(v_dram[bass.ds(b.t * P, P), :], vs[:, b.u2, :]).then_inc(b.ring(v_kept), 16)
                e = Tile(at, 5)
                if e.live:
                    e.wait_ring(sp, v_kept, 16)
                    carry(sp, sp_passed)
                    e.free(sp, summed, 4)
                    carry(sp, sp_passed)
                    for q in range(2):
                        for h in range(2):
                            sp.dma_start(VB[D * h:D * h + D, e.u4, q, D * h:D * h + D],
                                         v_dram[bass.ds(e.t * P + D * q, D), :]).then_inc(e.ring(v_spread), 16)
                f = Tile(at, 7)
                if f.live:
                    f.free(sp, y_added, 2)
                    carry(sp, sp_passed)
                    sp.dma_start(xt[:, f.u2, :], x[bass.ds(f.t * P, P), :]).then_inc(f.ring(x_in), 16)
                g = Tile(at, 10)
                if g.live:
                    g.wait(sp, x1_done)
                    carry(sp, sp_passed)
                    sp.dma_start(x1[bass.ds(g.t * P, P), :], xo[:, g.u2, :]).then_inc(g.ring(stored), 16)
            pipeline(sp, slot, tiles, LAG + 1, U)
            for k in stored:
                sp.wait_ge(k, 16 * tiles // 2)

        @block.tensor
        def _(pe):
            pe.wait_ge(loaded, 16 * NLOAD)
            nc.tensor.matmul(ps_qT, wqcT[:, :], wqup[:, :], start=True, stop=True)
            for c in range(4):
                g, f = c // 2, (c % 2) * P
                last = nc.tensor.matmul(ps_mT[:, c * P:(c + 1) * P], wogT[:, g, f:f + P], wout[:, g, :],
                                        start=True, stop=True)
            last.then_inc(prods, 1)
            pe.wait_ge(weights, 1)
            pe.wait_ge(made, 1)

            def slot(at):
                a, d, e, h, k = (Tile(at, n) for n in (0, 3, 4, 7, 8))
                if e.live:
                    e.wait(pe, qT_copied)
                    e.wait(pe, k_means)
                    e.free(pe, exped, 1)
                    for j in range(2):
                        nc.tensor.matmul(ps_S[:, j, :], idb[:, :], maskb[:, :], start=True, stop=False,
                                         skip_group_check=True)
                    for c in range(4):
                        for q in range(2):
                            last = nc.tensor.matmul(
                                ps_S[D * q:D * q + D, c // 2, (c % 2) * 2 * W:(c % 2 + 1) * 2 * W],
                                qT[:, e.u2, c, D * q:D * q + D],
                                KB[:, e.u2, q, :, :].rearrange("p h w -> p (h w)"),
                                start=False, stop=True, skip_group_check=True)
                    last.then_inc(scored, 1)
                if h.live:
                    h.wait(pe, mixed)
                    h.free(pe, PT_copied, 1)
                    for c in range(4):
                        last = nc.tensor.transpose(
                            ps_PT[:, c * P:(c + 1) * P],
                            Pm[:, h.u2, 2 * c:2 * c + 2, :].rearrange("p h d -> p (h d)"), idf[:, :])
                    last.then_inc(P_turned, 1)
                if d.live:
                    d.wait(pe, roped)
                    d.wait(pe, k_normed)
                    d.free(pe, qT_copied, 1)
                    d.free(pe, kT_copied, 1)
                    for c in range(4):
                        nc.tensor.transpose(ps_qT[:, c * P:(c + 1) * P],
                                            qk[:, d.u4, 2 * c:2 * c + 2, :].rearrange("p h d -> p (h d)"), idf[:, :])
                    nc.tensor.transpose(ps_kT, kd[:, d.u2, :, :].rearrange("p h d -> p (h d)"),
                                        idf[:, :]).then_inc(turned, 1)
                if k.live:
                    k.wait(pe, mT_copied)
                    k.free(pe, y_added, 1)
                    before = Tile(at, 1)
                    if before.live:
                        before.wait(pe, squared)
                    for c in range(4):
                        last = nc.tensor.matmul(ps_y, mT[:, c, :], wc[:, c, :], start=(c == 0), stop=(c == 3))
                    last.then_inc(y_done, 1)
                if a.live:
                    a.wait_ring(pe, xT_in, 16)
                    a.free(pe, squared, 1)
                    if k.live:
                        k.wait(pe, y_added)
                    nc.tensor.matmul(flat[:, 0:512], xTt[:, a.u2, :], wqkv[:, 0:512], start=True, stop=True)
                    nc.tensor.matmul(flat[:, 512:640], xTt[:, a.u2, :], wqkv[:, 512:640],
                                     start=True, stop=True).then_inc(projected, 1)
                if h.live:
                    h.wait(pe, PT_copied)
                    h.wait_ring(pe, v_spread, 64)
                    h.free(pe, mT_copied, 1)
                    for q in range(2):
                        last = nc.tensor.matmul(
                            ps_mT.rearrange("p (c t) -> p c t", c=4)[:, :, D * q:D * q + D],
                            VB[:, h.u4, q, :], PT[:, :, D * q:D * q + D], start=True, stop=True)
                    last.then_inc(summed, 1)
            pipeline(pe, slot, tiles, LAG, U)

        @block.scalar
        def _(act):
            act.wait_ge(prods, 1)
            nc.scalar.activation(wqkv[:, 0:512], ps_qT, ACT.Copy).then_inc(act_n, 1)
            nc.scalar.activation(wc[:, :, :].rearrange("p c n -> p (c n)"), ps_mT, ACT.Copy).then_inc(act_n, 1)
            act.wait_ge(act_n, 2)
            act.sem_inc(weights, 1)

            def slot(at):
                a, d, e, h = (Tile(at, n) for n in (0, 3, 4, 7))
                if h.live:
                    h.wait(act, P_turned)
                    h.free(act, summed, 1)
                    nc.scalar.activation(PT[:, :, :].rearrange("p c t -> p (c t)"), ps_PT,
                                         ACT.Copy).then_inc(PT_copied, 1)
                if d.live:
                    d.wait(act, turned)
                    d.free(act, scored, 2)
                    nc.scalar.activation(qT[:, d.u2, :, :].rearrange("p c t -> p (c t)"), ps_qT,
                                         ACT.Copy).then_inc(qT_copied, 1)
                    for g in range(2):
                        last = nc.scalar.activation(KB[D * g:D * g + D, d.u2, :, g, 0:D],
                                                    ps_kT[D * g:D * g + D, :].rearrange("p (b k) -> p b k", b=2),
                                                    ACT.Copy)
                    last.then_inc(kT_copied, 1)
                if e.live:
                    e.wait(act, maxed)
                    e.free(act, mixed, 4)
                    for g in range(H):
                        last = nc.scalar.activation(E[:, e.u4, g, :], ps_Sh[:, g // 4, g % 4, 0:D], ACT.Exp,
                                                    bias=nb[:, e.u2, g:g + 1], scale=sc8[:, e.u4, g:g + 1],
                                                    accum_out=Z[:, e.u2, g:g + 1])
                    last.then_inc(exped, 1)
                    e.wait(act, args)
                    e.wait(act, gate_args)
                    nc.scalar.activation(ex[:, e.u2, :, :], arg[:, e.u2, :, :], ACT.Exp).then_inc(small_exp, 1)
                if a.live:
                    a.wait(act, projected)
                    a.free(act, turned, 4)
                    nc.scalar.activation(qk[:, a.u4, :, :], ps_qk, ACT.Copy).then_inc(kq_copied, 1)
                    a.wait_ring(act, v_kept, 16, back=2)
                    nc.scalar.activation(vs[:, a.u2, :], ps_v, ACT.Copy).then_inc(v_copied, 1)
                    a.free(act, mean_sq, 2)
                    nc.scalar.activation(sq[:, a.u2, :, :], ps_qk, ACT.Square).then_inc(squared, 1)
                if h.live:
                    h.wait(act, summed)
                    h.free(act, y_done, 1)
                    nc.scalar.activation(mT[:, :, :].rearrange("p c t -> p (c t)"), ps_mT,
                                         ACT.Copy).then_inc(mT_copied, 1)
            pipeline(act, slot, tiles, LAG, U)

        @block.gpsimd
        def _(pool):
            n = Count(pool, pool_n)
            G = nc.gpsimd
            n.add(G.memset(halfneg[:, :], -0.5))
            n.add(G.memset(root[:, :], D ** -0.5))
            pool.wait_ge(loaded, 16 * NLOAD)
            n.add(G.tensor_scalar(nbg[:, :], bg[:, :], -1.0, None, ALU.mult))
            n.settle()

            def slot(at):
                b, e, f, k = (Tile(at, n) for n in (1, 4, 6, 8))
                if b.live:
                    b.wait(pool, kq_copied)
                    b.free(pool, roped, 1)
                    q = qk[:, b.u4, :, :]
                    G.tensor_tensor(tb[:, :, 0:16], q[:, :, 16:32],
                                    sin[:, 0:16].unsqueeze(1).to_broadcast([P, 9, 16]), ALU.mult)
                    G.tensor_tensor(tb[:, :, 16:32], q[:, :, 0:16],
                                    sin[:, 16:32].unsqueeze(1).to_broadcast([P, 9, 16]),
                                    ALU.mult).then_inc(sined, 1)
                if e.live:
                    e.wait(pool, scores_kept)
                    e.free(pool, small_exp, 2)
                    c = n.add(G.tensor_tensor(gl[:, :, :], s5[:, e.u2, :, 2:5],
                                              rinv[:, e.u4, 0:H].unsqueeze(2).to_broadcast([P, H, 3]), ALU.mult))
                    n.upto(c)
                    G.tensor_tensor(arg[:, e.u2, :, 4:7], nbg[:, :].unsqueeze(1).to_broadcast([P, H, 3]),
                                    gl[:, :, :], ALU.subtract).then_inc(gate_args, 1)
                if f.live:
                    f.wait(pool, mixing)
                    f.free(pool, P_turned, 2)
                    c = n.add(G.tensor_tensor(
                        Pm[:, f.u2, :, :], E[:, f.u4, :, :],
                        pa[:, f.u2, :].unsqueeze(2).to_broadcast([P, H, D]), ALU.mult))
                    n.upto(c)
                    Pv = Pm[:, f.u2, :, :].rearrange("p h (n k) -> p (h n) k", n=2)
                    G.tensor_tensor(
                        Pv, Pv, pc[:, f.u2, :, :].rearrange("p h n -> p (h n)").unsqueeze(2)
                        .to_broadcast([P, 2 * H, 32]), ALU.add).then_inc(mixed, 1)
                if k.live:
                    k.wait(pool, ln_var)
                    G.tensor_tensor(rs[:, k.u2, :], ve[:, k.u2, :], halfneg[:, 0:1], ALU.pow).then_inc(ln_rstd, 1)
                if b.live:
                    b.wait(pool, mean_sq)
                    b.free(pool, exped, 4)
                    G.tensor_tensor(rinv[:, b.u4, :], ms[:, b.u2, :], halfneg[:, 0:9], ALU.pow).then_inc(inv_rms, 1)
                    b.wait(pool, inv_rms)
                    G.tensor_tensor(sc8[:, b.u4, :], rinv[:, b.u4, 0:H], root[:, :], ALU.mult).then_inc(scales, 1)
            pipeline(pool, slot, tiles, LAG, U, [n])

        @block.vector
        def _(dve):
            n = Count(dve, dve_n)
            V = nc.vector
            n.add(V.memset(VB[:, :, :, :], 0.0))
            n.add(V.memset(KB[:, :, :, :, :], 0.0))
            dve.wait_ge(loaded, 16 * NLOAD)
            n.add(V.tensor_copy(idb[:, :], idf[:, :]))
            n.add(V.tensor_copy(maskb[:, :], maskf[:, :]))
            for h in range(2):
                n.add(V.tensor_tensor(gg[:, h, :], gq[:, :], gk[:, :], ALU.mult))
            n.add(V.tensor_scalar(wg[:, :], wgate[:, :], gqc[:, 0:1], None, ALU.mult))
            n.settle()
            for h in range(2):
                for i in range(2):
                    for q in range(2):
                        n.add(V.tensor_copy(KB[D * h:D * h + D, i, q, h, 66:69], wg[D * h:D * h + D, :]))
            n.settle()
            dve.sem_inc(made, 1)

            def slot(at):
                b, c, d, e, f, k, l = (Tile(at, m) for m in (1, 2, 3, 4, 5, 8, 9))
                if l.live:
                    l.wait(dve, ln_rstd)
                    l.wait_ring(dve, stored, 16, back=2)
                    V.tensor_scalar(xo[:, l.u2, :], r[:, l.u2, :], mv[:, l.u2, 0:1], rs[:, l.u2, 0:1],
                                    ALU.subtract, ALU.mult).then_inc(x1_done, 1)
                if e.live:
                    e.wait(dve, scored)
                    n_max = n.add(V.tensor_reduce(mx[:, :].rearrange("p (a h) -> p a h", a=2),
                                                  ps_Sh[:, :, :, 0:D], AX.X, ALU.max))
                    e.free(dve, gate_args, 2)
                    V.tensor_copy(s5[:, e.u2, :, :].rearrange("p (a h) w -> p a h w", a=2),
                                  ps_Sh[:, :, :, D:W]).then_inc(scores_kept, 1)
                    n.upto(n_max)
                    e.wait(dve, scales)
                    e.free(dve, exped, 2)
                    V.scalar_tensor_tensor(nb[:, e.u2, :], mx[:, :], -1.0, sc8[:, e.u4, :], ALU.mult,
                                           ALU.mult).then_inc(maxed, 1)
                if b.live:
                    b.wait(dve, kq_copied)
                    q = qk[:, b.u4, :, :]
                    n_ta = n.add(V.tensor_tensor(ta[:, :, :], q[:, :, 0:32],
                                                 cos[:, :].unsqueeze(1).to_broadcast([P, 9, 32]), ALU.mult))
                if e.live:
                    e.wait(dve, scores_kept)
                    n_un = n.add(V.scalar_tensor_tensor(
                        un[:, :, :], s5[:, e.u2, :, 0:2], 1.0 / 32,
                        sc8[:, e.u4, :].unsqueeze(2).to_broadcast([P, H, 2]), ALU.mult, ALU.mult))
                if k.live:
                    k.wait(dve, y_done)
                    k.wait_ring(dve, x_in, 16)
                    V.tensor_tensor(r[:, k.u2, :], ps_y, xt[:, k.u2, :], ALU.add).then_inc(y_added, 1)
                if e.live:
                    n.upto(n_un)
                    n_mc = n.add(V.tensor_tensor(mc[:, :], un[:, :, 0], un[:, :, 1], ALU.max))
                    e.wait(dve, maxed)
                    e.free(dve, small_exp, 2)
                    n.add(V.tensor_tensor(arg[:, e.u2, :, 3], snk[:, :], nb[:, e.u2, :], ALU.add))
                if k.live:
                    k.wait(dve, y_added)
                    n_bn = n.add(V.bn_stats(st[:, :], r[:, k.u2, :]))
                if e.live:
                    n.upto(n_mc)
                    n_mc = n.add(V.tensor_tensor(mc[:, :], mc[:, :], snk[:, :], ALU.max))
                if b.live:
                    n.upto(n_ta)
                    b.wait(dve, sined)
                    V.tensor_tensor(q[:, :, 0:32], ta[:, :, :], tb[:, :, :], ALU.add).then_inc(roped, 1)
                if e.live:
                    n.upto(n_mc)
                    n.add(V.tensor_tensor(arg[:, e.u2, :, 0:2], un[:, :, :],
                                          mc[:, :].unsqueeze(2).to_broadcast([P, H, 2]), ALU.subtract))
                    n_arg = n.add(V.tensor_tensor(arg[:, e.u2, :, 2], snk[:, :], mc[:, :], ALU.subtract))
                if k.live:
                    n.upto(n_bn)
                    carry(dve, dve_passed)
                    n_mv = n.add(V.bn_aggr(mv[:, k.u2, :], st[:, :]))
                if e.live:
                    n.upto(n_arg)
                    dve.sem_inc(args, 1)
                if d.live:
                    d.wait(dve, kT_copied)
                    V.tensor_reduce(KB[:, d.u2, :, :, 64:66],
                                    KB[:, d.u2, :, :, 0:D].rearrange("p b h (n k) -> p (b h) n k", n=2),
                                    AX.X, ALU.add).then_inc(k_means, 1)
                if c.live:
                    c.wait(dve, inv_rms)
                    c.wait(dve, roped)
                    c.free(dve, turned, 2)
                    V.scalar_tensor_tensor(kd[:, c.u2, :, :], qk[:, c.u4, 8:9, :].to_broadcast([P, 2, D]),
                                           rinv[:, c.u4, 8:9], gg[:, :, :], ALU.mult,
                                           ALU.mult).then_inc(k_normed, 1)
                if k.live:
                    n.upto(n_mv)
                    V.tensor_scalar(ve[:, k.u2, :], mv[:, k.u2, 1:2], 1e-5, None, ALU.add).then_inc(ln_var, 1)
                if f.live:
                    f.wait(dve, small_exp)
                    n.add(V.tensor_reduce(den[:, :, 2], ex[:, f.u2, :, 0:3], AX.X, ALU.add))
                    n.add(V.tensor_scalar(den[:, :, 3:6], ex[:, f.u2, :, 4:7], 1.0, None, ALU.add))
                    n.add(V.tensor_copy(den[:, :, 0], Z[:, f.u2, :]))
                    n_den = n.add(V.tensor_tensor(den[:, :, 1], Z[:, f.u2, :], ex[:, f.u2, :, 3], ALU.add))
                if b.live:
                    b.wait(dve, squared)
                    n_ss = n.add(V.tensor_reduce(ss[:, :], sq[:, b.u2, :, :], AX.X, ALU.add))
                if f.live:
                    n.upto(n_den)
                    n_rd = n.add(V.reciprocal(rd[:, :, :], den[:, :, :]))
                if b.live:
                    n.upto(n_ss)
                    b.free(dve, inv_rms, 2)
                    V.tensor_scalar(ms[:, b.u2, :], ss[:, :], 1.0 / D, 1e-6, ALU.mult, ALU.add).then_inc(mean_sq, 1)
                if f.live:
                    n.upto(n_rd)
                    n_gs = n.add(V.tensor_reduce(gs[:, :], rd[:, :, 3:6], AX.X, ALU.add))
                    n.add(V.tensor_tensor(a1[:, :], rd[:, :, 4], rd[:, :, 0], ALU.mult))
                    n_a2 = n.add(V.tensor_tensor(a2[:, :], rd[:, :, 5], rd[:, :, 1], ALU.mult))
                    n.upto(n_gs)
                    n_gs = n.add(V.tensor_scalar(gs[:, :], gs[:, :], 1e-6, None, ALU.max))
                    n.add(V.tensor_tensor(a3[:, :], rd[:, :, 2], rd[:, :, 3], ALU.mult))
                    n.upto(n_a2)
                    n.add(V.tensor_tensor(a1[:, :], a1[:, :], a2[:, :], ALU.add))
                    n.upto(n_gs)
                    n_rg = n.add(V.reciprocal(rg[:, :], gs[:, :]))
                if f.live:
                    n.upto(n_rg)
                    f.free(dve, mixed, 2)
                    n.add(V.tensor_tensor(pa[:, f.u2, :], a1[:, :], rg[:, :], ALU.mult))
                    n.add(V.tensor_tensor(a3[:, :], a3[:, :], rg[:, :], ALU.mult))
                    n.settle()
                    V.scalar_tensor_tensor(pc[:, f.u2, :, :], ex[:, f.u2, :, 0:2], 1.0 / 32,
                                           a3[:, :].unsqueeze(2).to_broadcast([P, H, 2]),
                                           ALU.mult, ALU.mult).then_inc(mixing, 1)
            pipeline(dve, slot, tiles, LAG, U, [n])

def cross_attention(nc, x1, ctxT, Wq, bq, Wk, bk, Wv, bv, Wo, bo, head_mask, ident, x2, tiles):
    H, D, T = 16, 8, 64
    LAG, U = 9, 4
    with ExitStack() as ctx:
        def sb(name, shape, dt=F32):
            return ctx.enter_context(nc.sbuf_tensor("x_" + name, shape, dt))

        def sem(name):
            return ctx.enter_context(nc.semaphore("x_" + name))

        wq, wk, wv, wo = (sb(n, [P, P]) for n in ("wq", "wk", "wv", "wo"))
        bqc, bkc, bvc = (sb(n, [P, 1]) for n in ("bqc", "bkc", "bvc"))
        bor, borow = sb("bor", [1, P]), sb("borow", [1, P])
        ones = sb("ones", [1, P])
        bob = sb("bob", [P, P])
        hm = sb("hm", [P, 4])
        idf = sb("idf", [P, P])
        halfneg = sb("halfneg", [P, 1])
        xa = sb("xa", [P, 2, P])
        ct = sb("ct", [P, 4, P])
        x1T = sb("x1T", [P, 2, P])
        qz = sb("qz", [P, 4, 4, P])
        kT = sb("kT", [P, 2, P])
        KB = sb("KB", [P, 2, 2, 4, T])
        VB = sb("VB", [P, 4, 2, 8, 64])
        mx = sb("mx", [P, H])
        sh = sb("sh", [P, 2, H, T])
        E = sb("E", [P, 2, H, T])
        PT = sb("PT", [P, 8, P])
        rz = sb("rz", [P, H])
        o = sb("o", [P, 2, P])
        oT = sb("oT", [P, 2, P])
        xb = sb("xb", [P, 2, P])
        xr = sb("xr", [P, 2, P])
        r = sb("r", [P, 2, P])
        st = sb("st", [P, 6])
        mv = sb("mv", [P, 2, 2])
        ve = sb("ve", [P, 2, 1])
        rs = sb("rs", [P, 2, 1])
        xo = sb("xo", [P, 2, P])

        ps = ctx.enter_context(nc.psum_tensor("x_ps", [P, 8, 512], F32))
        ps_x, ps_y = ps[:, 0, 0:P], ps[:, 0, P:2 * P]
        ps_q, ps_k, ps_oT = ps[:, 1, 0:P], ps[:, 1, P:2 * P], ps[:, 1, 2 * P:3 * P]
        ps_v = ps[:, 2, 0:2 * P].rearrange("p (b f) -> p b f", b=2)
        ps_S = ps[:, 3:5, :].rearrange("p a (h k) -> p (a h) k", k=T)
        ps_PT = ps[:, 5:7, :].rearrange("p a (c t) -> p (a c) t", t=P)
        ps_O = ps[:, 7, :].rearrange("p (c n) -> p c n", n=64)

        loaded, made, bias_sum, bias_row, bias_all = (sem(n) for n in ("loaded", "made", "bias_sum", "bias_row", "bias_all"))
        bias_done = sem("bias_done")
        xa_in, xb_in, stored = ([sem(f"{k}{i}") for i in range(2)] for k in ("xa_in", "xb_in", "stored"))
        ct_in = [sem(f"ct_in{i}") for i in range(4)]
        x_turned, x1T_ready, projected, q_ready, k_ready, v_ready = (
            sem(n) for n in ("x_turned", "x1T_ready", "projected", "q_ready", "k_ready", "v_ready"))
        k_spread, scored, shifted, exped = sem("k_spread"), sem("scored"), sem("shifted"), sem("exped")
        P_turned, PT_ready, summed, normed = sem("P_turned"), sem("PT_ready"), sem("summed"), sem("normed")
        o_turned, oT_ready, y_done, residual, y_added = (
            sem(n) for n in ("o_turned", "oT_ready", "y_done", "residual", "y_added"))
        ln_var, ln_rstd, x2_done = sem("ln_var"), sem("ln_rstd"), sem("x2_done")
        dve_n, act_n, pool_n = sem("dve_n"), sem("act_n"), sem("pool_n")
        sp_passed, dve_passed = sem("sp_passed"), sem("dve_passed")
        col = "(d a) -> d a"
        loads = [(wq[:, :], Wq), (wk[:, :], Wk), (wv[:, :], Wv), (wo[:, :], Wo),
                 (bqc[:, :], bq.rearrange(col, a=1)), (bkc[:, :], bk.rearrange(col, a=1)),
                 (bvc[:, :], bv.rearrange(col, a=1)), (bor[:, :], bo.rearrange("(a d) -> a d", a=1)),
                 (hm[:, :], head_mask), (idf[:, :], ident)]
        NLOAD = len(loads)
        block = ctx.enter_context(nc.Block())

        @block.sync
        def _(sp):
            for dst, src in loads:
                sp.dma_start(dst, src).then_inc(loaded, 16)

            def slot(at):
                a, h, l = (Tile(at, n) for n in (0, 7, 10))
                if a.live:
                    a.free(sp, x_turned, 2)
                    carry(sp, sp_passed)
                    sp.dma_start(xa[:, a.u2, :], x1[bass.ds(a.t * P, P), :]).then_inc(a.ring(xa_in), 16)
                    a.free(sp, projected, 4)
                    carry(sp, sp_passed)
                    sp.dma_start(ct[:, a.u4, :], ctxT[:, bass.ds(a.t * P, P)]).then_inc(a.ring(ct_in), 16)
                if h.live:
                    h.free(sp, residual, 2)
                    carry(sp, sp_passed)
                    sp.dma_start(xb[:, h.u2, :], x1[bass.ds(h.t * P, P), :]).then_inc(h.ring(xb_in), 16)
                if l.live:
                    l.wait(sp, x2_done)
                    carry(sp, sp_passed)
                    sp.dma_start(x2[bass.ds(l.t * P, P), :], xo[:, l.u2, :]).then_inc(l.ring(stored), 16)
            pipeline(sp, slot, tiles, LAG + 1, U)
            for k in stored:
                sp.wait_ge(k, 16 * tiles // 2)

        @block.tensor
        def _(pe):
            pe.wait_ge(loaded, 16 * NLOAD)
            nc.tensor.matmul(ps_x[0:1, :], bvc[:, :], wo[:, :], start=True, stop=True).then_inc(bias_sum, 1)
            pe.wait_ge(bias_row, 1)
            pe.wait_ge(made, 1)
            nc.tensor.matmul(ps_q, ones[:, :], borow[:, :], start=True, stop=True).then_inc(bias_all, 1)
            pe.wait_ge(bias_done, 1)

            def slot(at):
                a, b, d, f, h, k = (Tile(at, n) for n in (0, 1, 3, 5, 7, 8))
                if h.live:
                    h.wait(pe, normed)
                    h.free(pe, oT_ready, 1)
                    before = Tile(at, 2)
                    if before.live:
                        before.wait(pe, q_ready)
                        before.wait(pe, k_ready)
                    nc.tensor.transpose(ps_oT, o[:, h.u2, :], idf[:, :]).then_inc(o_turned, 1)
                if k.live:
                    k.wait(pe, oT_ready)
                    k.free(pe, y_added, 1)
                    before = Tile(at, 1)
                    if before.live:
                        before.wait(pe, x1T_ready)
                    nc.tensor.matmul(ps_y, oT[:, k.u2, :], wo[:, :], start=True, stop=True).then_inc(y_done, 1)
                if d.live:
                    d.wait(pe, q_ready)
                    d.wait(pe, k_spread)
                    d.free(pe, shifted, 1)
                    for g in range(4):
                        for q in range(2):
                            last = nc.tensor.matmul(
                                ps_S[T * q:T * q + T, 4 * g:4 * g + 4, :].rearrange("p h k -> p (h k)"),
                                qz[:, d.u4, g, T * q:T * q + T],
                                KB[:, d.u2, q, :, :].rearrange("p h k -> p (h k)"), start=True, stop=True)
                    last.then_inc(scored, 1)
                if f.live:
                    f.wait(pe, exped)
                    f.free(pe, PT_ready, 1)
                    for c in range(8):
                        last = nc.tensor.transpose(ps_PT[:, c, :],
                                                   E[:, f.u2, 2 * c:2 * c + 2, :].rearrange("p h k -> p (h k)"),
                                                   idf[:, :])
                    last.then_inc(P_turned, 1)
                if a.live:
                    a.wait_ring(pe, xa_in, 16)
                    a.free(pe, x1T_ready, 1)
                    if k.live:
                        k.wait(pe, y_added)
                    nc.tensor.transpose(ps_x, xa[:, a.u2, :], idf[:, :]).then_inc(x_turned, 1)
                if b.live:
                    b.wait(pe, x1T_ready)
                    b.wait_ring(pe, ct_in, 16)
                    b.free(pe, q_ready, 1)
                    b.free(pe, k_ready, 1)
                    b.free(pe, v_ready, 1)
                    if h.live:
                        h.wait(pe, oT_ready)
                    nc.tensor.matmul(ps_q, wq[:, :], x1T[:, b.u2, :], start=True, stop=True)
                    nc.tensor.matmul(ps_k, wk[:, :], ct[:, b.u4, :], start=True, stop=True)
                    for q in range(2):
                        for g in range(2):
                            last = nc.tensor.matmul(ps_v[T * g:T * g + T, q, :], ct[:, b.u4, T * q:T * q + T],
                                                    wv[:, :], start=True, stop=True)
                    last.then_inc(projected, 1)
                if f.live:
                    f.wait(pe, PT_ready)
                    f.wait(pe, v_ready)
                    f.free(pe, normed, 1)
                    for c in range(8):
                        for q in range(2):
                            last = nc.tensor.matmul(ps_O[T * q:T * q + T, c, :], PT[:, c, T * q:T * q + T],
                                                    VB[:, f.u4, q, c, :], start=True, stop=True)
                    last.then_inc(summed, 1)
            pipeline(pe, slot, tiles, LAG, U)

        @block.scalar
        def _(act):
            def slot(at):
                a, b, e, f, h = (Tile(at, n) for n in (0, 1, 4, 5, 7))
                if h.live:
                    h.wait(act, o_turned)
                    h.free(act, y_done, 2)
                    nc.scalar.activation(oT[:, h.u2, :], ps_oT, ACT.Copy).then_inc(oT_ready, 1)
                if e.live:
                    e.wait(act, shifted)
                    e.free(act, P_turned, 2)
                    nc.scalar.activation(E[:, e.u2, :, :], sh[:, e.u2, :, :], ACT.Exp,
                                         scale=D ** -0.5).then_inc(exped, 1)
                if f.live:
                    f.wait(act, P_turned)
                    f.free(act, summed, 1)
                    nc.scalar.activation(PT[:, :, :], ps_PT, ACT.Copy).then_inc(PT_ready, 1)
                if a.live:
                    a.wait(act, x_turned)
                    a.free(act, projected, 2)
                    nc.scalar.activation(x1T[:, a.u2, :], ps_x, ACT.Copy).then_inc(x1T_ready, 1)
                if b.live:
                    b.wait(act, projected)
                    b.free(act, scored, 4)
                    for g in range(4):
                        s = slice(32 * g, 32 * g + 32)
                        last = nc.scalar.activation(qz[s, b.u4, g, :], ps_q[s, :], ACT.Identity, bias=bqc[s, :])
                    last.then_inc(q_ready, 1)
                    b.free(act, k_spread, 2)
                    nc.scalar.activation(kT[:, b.u2, :], ps_k, ACT.Identity, bias=bkc[:, :]).then_inc(k_ready, 1)
                    b.free(act, summed, 4)
                    for g in range(2):
                        s = slice(T * g, T * g + T)
                        last = nc.scalar.activation(
                            VB[s, b.u4, :, :, D * g:D * g + D],
                            ps_v[s, :, :].rearrange("p b (c d) -> p b c d", d=2 * D)[:, :, :, D * g:D * g + D],
                            ACT.Copy)
                    last.then_inc(v_ready, 1)
            act.wait_ge(made, 1)
            pipeline(act, slot, tiles, LAG, U)

        @block.gpsimd
        def _(pool):
            nc.gpsimd.memset(halfneg[:, :], -0.5).then_inc(pool_n, 1)
            pool.wait_ge(pool_n, 1)
            pool.wait_ge(bias_done, 1)

            def slot(at):
                h, k = Tile(at, 7), Tile(at, 8)
                if k.live:
                    k.wait(pool, ln_var)
                    nc.gpsimd.tensor_tensor(rs[:, k.u2, :], ve[:, k.u2, :], halfneg[:, :],
                                            ALU.pow).then_inc(ln_rstd, 1)
                if h.live:
                    h.wait_ring(pool, xb_in, 16)
                    h.free(pool, y_added, 2)
                    nc.gpsimd.tensor_tensor(xr[:, h.u2, :], xb[:, h.u2, :], bob[:, :], ALU.add).then_inc(residual, 1)
            pipeline(pool, slot, tiles, LAG, U)

        @block.vector
        def _(dve):
            n = Count(dve, dve_n)
            V = nc.vector
            n.add(V.memset(qz[:, :, :, :], 0.0))
            n.add(V.memset(VB[:, :, :, :, :], 0.0))
            n.add(V.memset(ones[:, :], 1.0))
            n.settle()
            for g in range(2):
                n.add(V.memset(VB[T * g:T * g + T, :, :, :, 2 * D + g:2 * D + g + 1], 1.0))
            n.settle()
            dve.sem_inc(made, 1)
            dve.wait_ge(loaded, 16 * NLOAD)
            dve.wait_ge(bias_sum, 1)
            V.tensor_tensor(borow[:, :], ps_x[0:1, :], bor[:, :], ALU.add).then_inc(bias_row, 1)
            dve.wait_ge(bias_all, 1)
            V.tensor_copy(bob[:, :], ps_q).then_inc(bias_done, 1)

            def slot(at):
                c, d, g, k, l = (Tile(at, m) for m in (2, 3, 6, 8, 9))
                if l.live:
                    l.wait(dve, ln_rstd)
                    l.wait_ring(dve, stored, 16, back=2)
                    V.tensor_scalar(xo[:, l.u2, :], r[:, l.u2, :], mv[:, l.u2, 0:1], rs[:, l.u2, 0:1],
                                    ALU.subtract, ALU.mult).then_inc(x2_done, 1)
                if g.live:
                    g.wait(dve, summed)
                    n_rz = n.add(V.reciprocal(rz[:, :].rearrange("p (c h) -> p c h", h=2), ps_O[:, :, 16:18]))
                if k.live:
                    k.wait(dve, y_done)
                    k.wait(dve, residual)
                    V.tensor_tensor(r[:, k.u2, :], ps_y, xr[:, k.u2, :], ALU.add).then_inc(y_added, 1)
                if d.live:
                    d.wait(dve, scored)
                    n_mx = n.add(V.tensor_reduce(mx[:, :], ps_S, AX.X, ALU.max))
                if g.live:
                    n.upto(n_rz)
                    g.free(dve, o_turned, 2)
                    V.tensor_tensor(o[:, g.u2, :].rearrange("p (h d) -> p h d", d=D).rearrange("p (c h) d -> p c h d", h=2),
                                    ps_O[:, :, 0:16].rearrange("p c (h d) -> p c h d", d=D),
                                    rz[:, :].rearrange("p (c h) -> p c h", h=2).unsqueeze(3).to_broadcast([P, 8, 2, D]),
                                    ALU.mult).then_inc(normed, 1)
                if k.live:
                    k.wait(dve, y_added)
                    n_st = n.add(V.bn_stats(st[:, :], r[:, k.u2, :]))
                if d.live:
                    n.upto(n_mx)
                    d.free(dve, exped, 2)
                    V.tensor_tensor(sh[:, d.u2, :, :], ps_S, mx[:, :].unsqueeze(2).to_broadcast([P, H, T]),
                                    ALU.subtract).then_inc(shifted, 1)
                if k.live:
                    n.upto(n_st)
                    carry(dve, dve_passed)
                    n_mv = n.add(V.bn_aggr(mv[:, k.u2, :], st[:, :]))
                if c.live:
                    c.wait(dve, k_ready)
                    c.free(dve, scored, 2)
                    V.tensor_tensor(KB[:, c.u2, :, :, :],
                                    kT[:, c.u2, :].rearrange("p (b k) -> p b k", b=2).unsqueeze(2).to_broadcast([P, 2, 4, T]),
                                    hm[:, :].unsqueeze(1).unsqueeze(3).to_broadcast([P, 2, 4, T]),
                                    ALU.mult).then_inc(k_spread, 1)
                if k.live:
                    n.upto(n_mv)
                    V.tensor_scalar(ve[:, k.u2, :], mv[:, k.u2, 1:2], 1e-5, None, ALU.add).then_inc(ln_var, 1)
            pipeline(dve, slot, tiles, LAG, U, [n])

def experts(nc, x2, norm_scale, gate_w, gate_b, w1, b1, w2, b2, rank_table, ident, out, tiles):
    E, I, K = 8, 256, 2
    LAG, U = 2, 2
    N = K * P
    units = tiles // K
    with ExitStack() as ctx:
        def sb(name, shape, dt=F32):
            return ctx.enter_context(nc.sbuf_tensor("m_" + name, shape, dt))

        def sem(name):
            return ctx.enter_context(nc.semaphore("m_" + name))

        W1 = sb("W1", [P, E, 2, I])
        B1 = sb("B1", [P, E, 2, 2])
        B1l = sb("B1l", [P, E, 2])
        W2 = sb("W2", [P, E, 2, P])
        B2 = sb("B2", [E, P])
        ns = sb("ns", [P, 1])
        gw = sb("gw", [P, E])
        gb = sb("gb", [P, E])
        rt = sb("rt", [P, E])
        idf = sb("idf", [P, P])
        halfneg = sb("halfneg", [P, K])
        x = sb("x", [P, 2, K, P])
        sq = sb("sq", [P, K, P])
        ss = sb("ss", [P, 2, K])
        ms = sb("ms", [P, K])
        rr = sb("rr", [P, 2, K])
        t = sb("t", [P, K, P])
        tT = sb("tT", [P, 2, N])
        lg = sb("lg", [P, K, E])
        m1, m2, r1, r2, df = (sb(n_, [P, K]) for n_ in ("m1", "m2", "r1", "r2", "df"))
        eq, oh1, oh2, l2 = (sb(n_, [P, K, E]) for n_ in ("eq", "oh1", "oh2", "l2"))
        p1 = sb("p1", [P, K])
        p2 = sb("p2", [P, K])
        we = sb("we", [P, 2, K, E])
        wT = sb("wT", [E, K, P])
        acc = sb("acc", [P, 2, K, P])
        xg = sb("xg", [P, 4, 2, N])
        xl = sb("xl", [P, 4, 2, N])
        sg = sb("sg", [P, 4, 2, N])
        pr = sb("pr", [P, 2, 2, N])
        h = sb("h", [P, 4, 2, N])
        st = sb("st", [P, K, 6])
        mv = sb("mv", [P, 2, K, 2])
        ve = sb("ve", [P, 2, K])
        rs = sb("rs", [P, 2, K])
        xo = sb("xo", [P, 2, K, P])

        ps = ctx.enter_context(nc.psum_tensor("m_ps", [P, 8, 512], F32))
        ps_g = ps[:, 0:2, :].rearrange("p a (j n) -> p a j n", j=2)
        ps_l = ps[:, 2:4, :].rearrange("p a (j n) -> p a j n", j=2)
        ps_y = ps[:, 4:6, 0:N].rearrange("p a (k n) -> p a k n", k=K)
        ps_t = ps[:, 6, 0:N]
        ps_lg = ps[:, 7, 0:K * E].rearrange("p (k e) -> p k e", e=E)
        ps_wT = ps[0:E, 6, N:2 * N].rearrange("p (k n) -> p k n", k=K)
        ps_b = ps[:, 7, N:2 * N].rearrange("p (k n) -> p k n", k=K)

        loaded, made = sem("loaded"), sem("made")
        x_in, stored = ([sem(f"{k}{i}") for i in range(2)] for k in ("x_in", "stored"))
        squared, mean_sq, inv_rms, normed, t_turned, tT_ready = (
            sem(k) for k in ("squared", "mean_sq", "inv_rms", "normed", "t_turned", "tT_ready"))
        logits, logit_gap, shares, routed, w_turned, wT_ready, biased, acc_ready = (
            sem(k) for k in ("logits", "logit_gap", "shares", "routed", "w_turned", "wT_ready", "biased", "acc_ready"))
        up, glu_ready, lin_ready, clipped, gated, prod_ready, act_ready, down, added = (
            sem(k) for k in ("up", "glu_ready", "lin_ready", "clipped", "gated", "prod_ready", "act_ready", "down", "added"))
        ln_var, ln_rstd, out_done = sem("ln_var"), sem("ln_rstd"), sem("out_done")
        dve_n, pool_n = sem("dve_n"), sem("pool_n")
        sp_passed, dve_passed = sem("sp_passed"), sem("dve_passed")
        loads = [(W1[:, :, :, :], w1), (W2[:, :, :, :], w2), (B1[:, :, :, :], b1), (B2[:, :], b2),
                 (ns[:, :], norm_scale.rearrange("(d a) -> d a", a=1)), (gw[:, :], gate_w),
                 (gb[:, :], gate_b.partition_broadcast(P)), (rt[:, :], rank_table), (idf[:, :], ident)]
        NLOAD = len(loads)

        def step(eng, tile, sem_, e, back=0):
            if not tile.static or tile.t * E + e >= back:
                eng.wait_ge(sem_, tile.t * E + (e + 1 - back))

        block = ctx.enter_context(nc.Block())

        @block.sync
        def _(sp):
            for dst, src in loads:
                sp.dma_start(dst, src).then_inc(loaded, 16)

            def slot(at):
                a, d = Tile(at, 0), Tile(at, 3)
                if a.live:
                    a.free(sp, acc_ready, 2)
                    carry(sp, sp_passed)
                    sp.dma_start(x[:, a.u2, :, :], x2[bass.ds(a.t * N, N), :].rearrange("(k p) d -> p k d", p=P))\
                        .then_inc(a.ring(x_in), 16)
                if d.live:
                    d.wait(sp, out_done)
                    carry(sp, sp_passed)
                    sp.dma_start(out[bass.ds(d.t * N, N), :].rearrange("(k p) d -> p k d", p=P), xo[:, d.u2, :, :])\
                        .then_inc(d.ring(stored), 16)
            pipeline(sp, slot, units, LAG + 1, U)
            for k in stored:
                sp.wait_ge(k, 16 * units // 2)

        @block.tensor
        def _(pe):
            pe.wait_ge(loaded, 16 * NLOAD)

            def slot(at):
                a, b, c = (Tile(at, n_) for n_ in (0, 1, 2))
                for e in range(E):
                    if b.live:
                        if e == 0:
                            b.wait(pe, tT_ready)
                        step(pe, b, glu_ready, e, 2)
                        step(pe, b, lin_ready, e, 2)
                        for j in range(2):
                            nc.tensor.matmul(ps_g[:, e % 2, j, :], W1[:, e, 0, j * P:(j + 1) * P], tT[:, b.u2, :],
                                             start=True, stop=True)
                        for j in range(2):
                            last = nc.tensor.matmul(ps_l[:, e % 2, j, :], W1[:, e, 1, j * P:(j + 1) * P],
                                                    tT[:, b.u2, :], start=True, stop=True)
                        last.then_inc(up, 1)
                    if a.live and e == 3:
                        a.wait(pe, normed)
                        a.free(pe, wT_ready, 1)
                        a.free(pe, tT_ready, 1)
                        for k in range(K):
                            last = nc.tensor.transpose(ps_t[:, k * P:(k + 1) * P], t[:, k, :], idf[:, :])
                        last.then_inc(t_turned, 1)
                    if a.live and e == 5:
                        a.wait(pe, tT_ready)
                        a.free(pe, acc_ready, 1)
                        for k in range(K):
                            last = nc.tensor.matmul(ps_lg[:, k, :], tT[:, a.u2, k * P:(k + 1) * P], gw[:, :],
                                                    start=True, stop=True)
                        last.then_inc(logits, 1)
                    if b.live and e == 1:
                        b.wait(pe, routed)
                        for k in range(K):
                            last = nc.tensor.transpose(ps_wT[:, k, :], we[:, b.u2, k, :], idf[:, :])
                        last.then_inc(w_turned, 1)
                    if b.live and e == 3:
                        b.wait(pe, wT_ready)
                        for k in range(K):
                            last = nc.tensor.matmul(ps_b[:, k, :], wT[:, k, :], B2[:, :], start=True, stop=True)
                        last.then_inc(biased, 1)
                    o, oe = (b, e - 3) if e >= 3 else (c, e + 5)
                    if o.live:
                        step(pe, o, act_ready, oe)
                        step(pe, o, added, oe, 2)
                        for k in range(K):
                            for j in range(2):
                                last = nc.tensor.matmul(ps_y[:, oe % 2, k, :], h[:, oe % 4, j, k * P:(k + 1) * P],
                                                        W2[:, oe, j, :], start=(j == 0), stop=(j == 1))
                        last.then_inc(down, 1)
            pipeline(pe, slot, units, LAG, U)

        @block.scalar
        def _(act):
            act.wait_ge(made, 1)

            def slot(at):
                a, b = Tile(at, 0), Tile(at, 1)
                for e in range(E):
                    if a.live and e == 0:
                        a.wait_ring(act, x_in, 16)
                        a.free(act, mean_sq, 2)
                        for k in range(K):
                            last = nc.scalar.activation(sq[:, k, :], x[:, a.u2, k, :], ACT.Square,
                                                        accum_out=ss[:, a.u2, k:k + 1])
                        last.then_inc(squared, 1)
                    if b.live:
                        step(act, b, up, e)
                        step(act, b, prod_ready, e, 4)
                        for j in range(2):
                            last = nc.scalar.activation(xl[:, e % 4, j, :], ps_l[:, e % 2, j, :], ACT.Identity,
                                                        bias=B1l[:, e, j:j + 1])
                        last.then_inc(lin_ready, 1)
                    if a.live and e == 4:
                        a.wait(act, t_turned)
                        a.free(act, up, 2, E)
                        nc.scalar.activation(tT[:, a.u2, :], ps_t, ACT.Copy, scale=ns[:, :]).then_inc(tT_ready, 1)
                    if a.live and e == 7:
                        a.wait(act, logit_gap)
                        a.free(act, routed, 1)
                        nc.scalar.activation(p1[:, :], df[:, :], ACT.Sigmoid).then_inc(shares, 1)
                        nc.scalar.activation(p2[:, :], df[:, :], ACT.Sigmoid, scale=-1.0).then_inc(shares, 1)
                    if b.live:
                        step(act, b, glu_ready, e)
                        step(act, b, act_ready, e, 4)
                        nc.scalar.activation(sg[:, e % 4, :, :], xg[:, e % 4, :, :], ACT.Sigmoid,
                                             scale=1.702).then_inc(gated, 1)
            pipeline(act, slot, units, LAG, U)

        @block.gpsimd
        def _(pool):
            nc.gpsimd.memset(halfneg[:, :], -0.5).then_inc(pool_n, 1)
            pool.wait_ge(pool_n, 1)

            def slot(at):
                a, b, d = (Tile(at, n_) for n_ in (0, 1, 2))
                for e in range(E):
                    if a.live and e == 1:
                        a.wait(pool, mean_sq)
                        a.free(pool, normed, 2)
                        nc.gpsimd.tensor_tensor(rr[:, a.u2, :], ms[:, :], halfneg[:, :], ALU.pow).then_inc(inv_rms, 1)
                    if d.live and e == 6:
                        d.wait(pool, ln_var)
                        d.free(pool, out_done, 2)
                        nc.gpsimd.tensor_tensor(rs[:, d.u2, :], ve[:, d.u2, :], halfneg[:, :],
                                                ALU.pow).then_inc(ln_rstd, 1)
                    if b.live:
                        step(pool, b, glu_ready, e)
                        step(pool, b, clipped, e)
                        step(pool, b, act_ready, e, 2)
                        nc.gpsimd.tensor_tensor(pr[:, e % 2, :, :], xg[:, e % 4, :, :], xl[:, e % 4, :, :],
                                                ALU.mult).then_inc(prod_ready, 1)
                    o, oe = (b, e - 1) if e >= 1 else (d, 7)
                    if o.live:
                        step(pool, o, gated, oe)
                        step(pool, o, down, oe, 4)
                        step(pool, o, prod_ready, oe)
                        nc.gpsimd.tensor_tensor(h[:, oe % 4, :, :], pr[:, oe % 2, :, :], sg[:, oe % 4, :, :],
                                                ALU.mult).then_inc(act_ready, 1)
            pipeline(pool, slot, units, LAG, U)

        @block.vector
        def _(dve):
            n = Count(dve, dve_n)
            V = nc.vector
            dve.wait_ge(loaded, 16 * NLOAD)
            V.tensor_scalar(B1l[:, :, :], B1[:, :, 1, :], 1.0, None, ALU.add).then_inc(made, 1)

            def slot(at):
                a, b, c = (Tile(at, m) for m in (0, 1, 2))
                d = c

                def route(e, step_):
                    bc = lambda v: v.unsqueeze(2).to_broadcast([P, K, E])
                    rb = rt[:, :].unsqueeze(1).to_broadcast([P, K, E])
                    at_ = (e, step_)
                    if at_ == (0, 0):
                        a.wait(dve, squared)
                        a.free(dve, inv_rms, 1)
                        V.tensor_scalar(ms[:, :], ss[:, a.u2, :], 1.0 / P, 1e-5, ALU.mult, ALU.add).then_inc(mean_sq, 1)
                    if at_ == (2, 0):
                        a.wait(dve, inv_rms)
                        a.free(dve, t_turned, 1)
                        for k in range(K):
                            last = V.tensor_scalar(t[:, k, :], x[:, a.u2, k, :], rr[:, a.u2, k:k + 1], None, ALU.mult)
                        last.then_inc(normed, 1)
                    if at_ == (5, 0):
                        a.wait(dve, logits)
                        n.add(V.tensor_tensor(lg[:, :, :], ps_lg, gb[:, :].unsqueeze(1).to_broadcast([P, K, E]),
                                              ALU.add))
                    if at_ == (5, 1):
                        n.settle()
                        n.add(V.tensor_reduce(m1[:, :], lg[:, :, :], AX.X, ALU.max))
                    if at_ == (5, 2):
                        n.settle()
                        for k in range(K):
                            n.add(V.scalar_tensor_tensor(eq[:, k, :], lg[:, k, :], m1[:, k:k + 1], rt[:, :],
                                                         ALU.is_equal, ALU.mult))
                    if at_ == (6, 0):
                        n.settle()
                        n.add(V.tensor_reduce(r1[:, :], eq[:, :, :], AX.X, ALU.max))
                    if at_ == (6, 1):
                        n.settle()
                        n.add(V.tensor_tensor(oh1[:, :, :], rb, bc(r1[:, :]), ALU.is_equal))
                        n.settle()
                        n.add(V.scalar_tensor_tensor(l2[:, :, :], oh1[:, :, :], -3.0e38, lg[:, :, :], ALU.mult, ALU.add))
                    if at_ == (6, 2):
                        n.settle()
                        n.add(V.tensor_reduce(m2[:, :], l2[:, :, :], AX.X, ALU.max))
                    if at_ == (7, 0):
                        n.settle()
                        V.tensor_tensor(df[:, :], m1[:, :], m2[:, :], ALU.subtract).then_inc(logit_gap, 1)
                        for k in range(K):
                            n.add(V.scalar_tensor_tensor(eq[:, k, :], l2[:, k, :], m2[:, k:k + 1], rt[:, :],
                                                         ALU.is_equal, ALU.mult))
                    if at_ == (7, 1):
                        n.settle()
                        n.add(V.tensor_reduce(r2[:, :], eq[:, :, :], AX.X, ALU.max))
                    if at_ == (7, 2):
                        n.settle()
                        a.wait(dve, shares, 2)
                        for k in range(K):
                            n.add(V.tensor_scalar(oh1[:, k, :], rt[:, :], r1[:, k:k + 1], p1[:, k:k + 1],
                                                  ALU.is_equal, ALU.mult))
                            n.add(V.tensor_scalar(oh2[:, k, :], rt[:, :], r2[:, k:k + 1], p2[:, k:k + 1],
                                                  ALU.is_equal, ALU.mult))
                        n.settle()
                        V.tensor_tensor(we[:, a.u2, :, :], oh1[:, :, :], oh2[:, :, :], ALU.add).then_inc(routed, 1)

                for e in range(E):
                    if b.live:
                        step(dve, b, up, e)
                        step(dve, b, gated, e, 4)
                        step(dve, b, prod_ready, e, 4)
                        for j in range(2):
                            last = V.tensor_scalar(xg[:, e % 4, j, :], ps_g[:, e % 2, j, :], B1[:, e, 0, j:j + 1], 7.0,
                                                   ALU.add, ALU.min)
                        last.then_inc(glu_ready, 1)
                    if a.live:
                        route(e, 0)
                    if b.live and e == 1:
                        b.wait(dve, w_turned)
                        V.tensor_copy(wT[:, :, :], ps_wT).then_inc(wT_ready, 1)
                    if b.live:
                        step(dve, b, lin_ready, e)
                        V.tensor_scalar(xl[:, e % 4, :, :], xl[:, e % 4, :, :], 8.0, -6.0, ALU.min,
                                        ALU.max).then_inc(clipped, 1)
                    if a.live:
                        route(e, 1)
                    if b.live and e == 3:
                        b.wait(dve, biased)
                        b.free(dve, out_done, 2)
                        V.scalar_tensor_tensor(acc[:, b.u2, :, :], x[:, b.u2, :, :], 2.0, ps_b, ALU.mult,
                                               ALU.add).then_inc(acc_ready, 1)
                    o, oe = (b, e - 4) if e >= 4 else (c, e + 4)
                    if o.live:
                        step(dve, o, down, oe)
                        if oe == 0:
                            o.wait(dve, acc_ready)
                        else:
                            step(dve, o, added, oe, 1)
                        for k in range(K):
                            last = V.scalar_tensor_tensor(acc[:, o.u2, k, :], ps_y[:, oe % 2, k, :],
                                                          we[:, o.u2, k, oe:oe + 1], acc[:, o.u2, k, :],
                                                          ALU.mult, ALU.add)
                        last.then_inc(added, 1)
                    if a.live:
                        route(e, 2)
                    if c.live and e == 4:
                        step(dve, c, added, E - 1)
                        for k in range(K):
                            n.add(V.bn_stats(st[:, k, :], acc[:, c.u2, k, :]))
                    if c.live and e == 5:
                        n.settle()
                        carry(dve, dve_passed)
                        for k in range(K):
                            n.add(V.bn_aggr(mv[:, c.u2, k, :], st[:, k, :]))
                    if c.live and e == 6:
                        n.settle()
                        V.tensor_scalar(ve[:, c.u2, :], mv[:, c.u2, :, 1], 1e-5, None, ALU.add).then_inc(ln_var, 1)
                    if c.live and e == 7:
                        c.wait(dve, ln_rstd)
                        c.wait_ring(dve, stored, 16, back=2)
                        for k in range(K):
                            last = V.tensor_scalar(xo[:, c.u2, k, :], acc[:, c.u2, k, :], mv[:, c.u2, k, 0:1],
                                                   rs[:, c.u2, k:k + 1], ALU.subtract, ALU.mult)
                        last.then_inc(out_done, 1)
            pipeline(dve, slot, units, LAG, U, [n])


def build(nc, ap, out):
    rows = ap["x"].shape[0]
    tiles = rows // P

    def scratch(name, width):
        return nc.dram_tensor(name, (rows, width), F32, kind="Internal").ap()

    v_dram, x1, x2 = scratch("v_dram", T), scratch("x1_dram", P), scratch("x2_dram", P)
    attention(nc, *(ap[k] for k in (
        "x", "xT", "w_qcT", "w_qup", "w_k", "w_v", "g_q", "g_k", "w_gate", "b_gate", "sink", "w_ogT", "w_out",
        "rope_cos", "rope_sin", "mask", "ident")), v_dram, x1, tiles)
    cross_attention(nc, x1, *(ap[k] for k in (
        "ctxT", "Wq", "bq", "Wk", "bk", "Wv", "bv", "Wo", "bo", "head_mask", "ident")), x2, tiles)
    experts(nc, x2, *(ap[k] for k in (
        "norm_scale", "gate_w", "gate_b", "w1", "b1", "w2", "b2", "rank_table", "ident")), out, tiles)


def rope_tables():
    half = 16
    inv = (np.float32(1.0) / np.float32(10000.0) ** (np.arange(half, dtype=np.float32) * np.float32(2.0) / np.float32(32))).astype(np.float32)
    ang = np.arange(T, dtype=np.float32)[:, None] * inv[None, :]
    c, s = np.cos(ang).astype(np.float32), np.sin(ang).astype(np.float32)
    return np.tile(np.concatenate([c, c], 1), (2, 1)), np.tile(np.concatenate([-s, s], 1), (2, 1))


def mask_table():
    q = np.arange(P)[:, None] % T
    k = np.arange(T)[None, :]
    keys = np.where(k <= q, 0.0, NEG)
    blocks = np.where((np.arange(2)[None, :] + 1) * 32 - 1 <= q, 0.0, NEG)
    one = np.concatenate([keys, blocks, np.zeros((P, 3))], 1)
    return np.tile(one, (1, 4)).astype(np.float32)


def head_mask_table():
    return (np.arange(P)[:, None] // 8 % 4 == np.arange(4)[None, :]).astype(np.float32)


def rank_table():
    return np.broadcast_to(8.0 - np.arange(8), (P, 8)).astype(np.float32)


_OUT = (64, 64, 128)


def kernel(**inputs):
    import concourse.bacc as bacc
    from concourse.bass_utils import run_bass_kernel_spmd

    g = {k: np.asarray(v) for k, v in inputs.items()}
    x = g["x"].reshape(-1, P)
    cos, sin = rope_tables()
    arrays = {
        "x": x, "xT": x.T, "ctxT": g["ctx_1024"].reshape(-1, P).T,
        "w_qcT": g["L0_attn_w_qc"].T, "w_ogT": g["L0_attn_w_out_group"].transpose(0, 2, 1),
        "w1": g["L0_ffn_mlp1_w"].reshape(8, P, 256, 2).transpose(1, 0, 3, 2),
        "b1": g["L0_ffn_mlp1_b"].reshape(8, 2, P, 2).transpose(2, 0, 3, 1),
        "w2": g["L0_ffn_mlp2_w"].reshape(8, 2, P, P).transpose(2, 0, 1, 3),
        "rope_cos": cos, "rope_sin": sin, "mask": mask_table(), "head_mask": head_mask_table(),
        "rank_table": rank_table(), "ident": np.eye(P, dtype=np.float32),
    }
    for new, old in (("w_qup", "attn_w_qup"), ("w_k", "attn_w_k"), ("w_v", "attn_w_v"), ("g_q", "attn_g_qnorm"),
                     ("g_k", "attn_g_knorm"), ("w_gate", "attn_w_gate"), ("b_gate", "attn_b_gate"),
                     ("sink", "attn_sink_logit"), ("w_out", "attn_w_out"), ("Wq", "xattn_Wq"), ("bq", "xattn_bq"),
                     ("Wk", "xattn_Wk"), ("bk", "xattn_bk"), ("Wv", "xattn_Wv"), ("bv", "xattn_bv"),
                     ("Wo", "xattn_Wo"), ("bo", "xattn_bo"), ("norm_scale", "ffn_norm_scale"),
                     ("gate_w", "ffn_gate_w"), ("gate_b", "ffn_gate_b"), ("b2", "ffn_mlp2_b")):
        arrays[new] = g["L0_" + old]
    arrays = {k: np.ascontiguousarray(v) for k, v in arrays.items()}
    nc = bacc.Bacc("TRN2", target_bir_lowering=False, num_devices=1)
    ap = {k: nc.dram_tensor(f"in_{k}", v.shape, mybir.dt.from_np(v.dtype), kind="ExternalInput").ap()
          for k, v in arrays.items()}
    out = nc.dram_tensor("out_x", (x.shape[0], P), F32, kind="ExternalOutput").ap()
    build(nc, ap, out)
    r = run_bass_kernel_spmd(nc, [{f"in_{k}": v for k, v in arrays.items()}], core_ids=[0])
    return r.results[0]["out_x"].reshape(_OUT)
```

```python
import numpy as np
import concourse.bass as bass
from concourse import mybir
from concourse.alu_op_type import AluOpType as ALU
from contextlib import ExitStack

F32 = mybir.dt.float32
BF16 = mybir.dt.bfloat16
F32R = mybir.dt.float32r
U32 = mybir.dt.uint32
HIGH = 0xFFFFF000
ACT = mybir.ActivationFunctionType
AX = mybir.AxisListType
P = 128
T = 64
NEG = -1.0e30


class Count:

    def __init__(self, eng, sem):
        self.eng, self.sem, self.n, self.shift = eng, sem, 0, None

    def add(self, ins):
        self.n += 1
        ins.then_inc(self.sem, 1)
        return self.n

    def upto(self, n):
        self.eng.wait_ge(self.sem, n if self.shift is None else self.shift + n)

    def settle(self):
        self.upto(self.n)


class Tile:

    def __init__(self, at, lag):
        i, u, unroll, tiles = at
        self.i, self.c, self.unroll = i, u - lag, unroll
        self.static = isinstance(i, int)
        self.t = i * unroll + self.c
        self.live = not self.static or 0 <= self.t < tiles
        self.u2, self.u4 = self.c % 2, self.c % 4

    def wait(self, eng, sem, per=1):
        eng.wait_ge(sem, (self.t + 1) * per)

    def free(self, eng, sem, ahead, per=1):
        if not self.static or self.t >= ahead:
            eng.wait_ge(sem, (self.t + 1 - ahead) * per)

    def ring(self, sems, back=0):
        return sems[(self.c - back) % len(sems)]

    def wait_ring(self, eng, sems, per, back=0):
        if not self.static or self.t >= back:
            n = len(sems)
            eng.wait_ge(self.ring(sems, back), (self.i * (self.unroll // n) + (self.c - back) // n + 1) * per)


def carry(eng, passed):
    eng.sem_inc(passed, 1)


def pipeline(eng, slot, tiles, lags, unroll, counts=()):
    first = -(-(lags + 2) // unroll)
    for s in range(first * unroll):
        before = [c.n for c in counts]
        slot((s // unroll, s % unroll, unroll, tiles))
    per = [unroll * (c.n - b) for c, b in zip(counts, before)]
    rounds = tiles // unroll
    assert tiles % unroll == 0 and rounds > first
    start = [c.n for c in counts]
    with eng.Fori(first, rounds) as i:
        for c, p in zip(counts, per):
            c.shift = (i - first) * p
        for u in range(unroll):
            slot((i, u, unroll, tiles))
    for c, p, b in zip(counts, per, start):
        assert c.n - b == p, (c.n - b, p)
        c.n, c.shift = b + p * (rounds - first), None
    for s in range(tiles, tiles + lags):
        slot((s // unroll, s % unroll, unroll, tiles))


TABLES = {"table": 2 * 64 + 2 * 64 + 1 + 3 + 3 + 8 + 32 + 32 + 4 * 69 + P, "table64": 512 + 2 * P, "table32": P + 512}


def columns(ap, *widths):
    ends = [sum(widths[:i + 1]) for i in range(len(widths))]
    return [ap[:, e - w:e] for e, w in zip(ends, widths)]


def attention(nc, x, xT, table, table64, table32, v_dram, x1, tiles, later):
    H, D, W = 8, 64, 69
    GW = 4 * W
    LAG, U = 9, 4
    with ExitStack() as ctx:
        def sb(name, shape, dt=F32):
            return ctx.enter_context(nc.sbuf_tensor("a_" + name, shape, dt))

        def sem(name):
            return ctx.enter_context(nc.semaphore("a_" + name))

        tab = sb("tab", [P, 512 + TABLES["table"]])
        tab64 = sb("tab64", [D, TABLES["table64"]])
        tab32 = sb("tab32", [32, TABLES["table32"]])
        wqkv = tab[:, 0:640]
        gq, gk, gqc, wgate, bg, snk, cos, sin, maskf, idf = columns(
            tab[:, 640:], D, D, 1, 3, 3, H, 32, 32, GW, P)
        wogT, wout = (v.rearrange("p (g f) -> p g f", g=2) for v in columns(tab64[:, :], 512, 2 * P))
        wqcT, wqup = columns(tab32[:, :], P, H * D)
        wc = sb("wc", [P, 4, P])
        gg = sb("gg", [P, 2, D])
        wg = sb("wg", [P, 3])
        maskb = sb("maskb", [P, GW], BF16)
        idb = sb("idb", [P, P], BF16)
        halfneg = sb("halfneg", [P, 16])
        root = sb("root", [P, H])
        xTt = sb("xTt", [P, 2, P])
        xt = sb("xt", [P, 2, P])
        qk = sb("qk", [P, 4, 9, D])
        sq = sb("sq", [P, 2, 9, D])
        ta = sb("ta", [P, 9, 32])
        tb = sb("tb", [P, 9, 32])
        ss = sb("ss", [P, 9])
        ms = sb("ms", [P, 2, 9])
        rinv = sb("rinv", [P, 4, 9])
        kd = sb("kd", [P, 2, 2, D])
        vs = sb("vs", [P, 2, D])
        VB = sb("VB", [P, 4, 2, P])
        qT = sb("qT", [P, 2, 4, P])
        KB = sb("KB", [P, 2, 2, 2, W])
        mx = sb("mx", [P, H])
        s5 = sb("s5", [P, 2, H, 5])
        sc8 = sb("sc8", [P, 4, H])
        gl = sb("gl", [P, H, 3])
        nbg = sb("nbg", [P, 3])
        Z = sb("Z", [P, 2, H])
        a3 = sb("a3", [P, H])
        nb = sb("nb", [P, 2, H])
        un = sb("un", [P, H, 2])
        mc = sb("mc", [P, H])
        arg = sb("arg", [P, 2, H, 7])
        ex = sb("ex", [P, 2, H, 7])
        den = sb("den", [P, H, 6])
        rd = sb("rd", [P, H, 6])
        gs = sb("gs", [P, H])
        rg = sb("rg", [P, H])
        a1 = sb("a1", [P, H])
        a2 = sb("a2", [P, H])
        pa = sb("pa", [P, 2, H])
        pc = sb("pc", [P, 2, H, 2])
        E = sb("E", [P, 4, H, D])
        Pm = sb("Pm", [P, 2, H, D])
        PT = sb("PT", [P, 4, P])
        mT = sb("mT", [P, 4, P])
        r = sb("r", [P, 2, P])
        st = sb("st", [P, 6])
        mv = sb("mv", [P, 2, 2])
        ve = sb("ve", [P, 2, 1])
        rs = sb("rs", [P, 2, 1])
        xo = sb("xo", [P, 2, P])

        ps = ctx.enter_context(nc.psum_tensor("a_ps", [P, 8, 512], F32))
        flat = ps[:, 0:2, :].rearrange("p a b -> p (a b)")
        ps_qk = flat[:, 0:9 * D].rearrange("p (h d) -> p h d", d=D)
        ps_v = flat[:, 9 * D:10 * D]
        ps_y = ps[:, 1, 256:256 + P]
        ps_qT, ps_kT = ps[:, 2, :], ps[:, 3, 0:P]
        ps_S = ps[:, 4:6, 0:GW]
        ps_Sh = ps_S.rearrange("p a (h w) -> p a h w", w=W)
        ps_PT, ps_mT = ps[:, 6, :], ps[:, 7, :]

        loaded = sem("loaded")
        made = sem("made")
        prods = sem("prods")
        weights = sem("weights")
        xT_in, x_in, stored = ([sem(f"{k}{i}") for i in range(2)] for k in ("xT_in", "x_in", "stored"))
        v_spread, v_kept = ([sem(f"{k}{i}") for i in range(4)] for k in ("v_spread", "v_kept"))
        sined, scores_kept, gate_args, scales = sem("sined"), sem("scores_kept"), sem("gate_args"), sem("scales")
        projected, kq_copied, squared, v_copied = sem("projected"), sem("kq_copied"), sem("squared"), sem("v_copied")
        roped, mean_sq, inv_rms, k_normed = sem("roped"), sem("mean_sq"), sem("inv_rms"), sem("k_normed")
        turned, qT_copied, kT_copied, k_means = sem("turned"), sem("qT_copied"), sem("kT_copied"), sem("k_means")
        scored, maxed, exped, args, small_exp = sem("scored"), sem("maxed"), sem("exped"), sem("args"), sem("small_exp")
        mixing, mixed, P_turned, PT_copied = sem("mixing"), sem("mixed"), sem("P_turned"), sem("PT_copied")
        summed, mT_copied, y_done, y_added = sem("summed"), sem("mT_copied"), sem("y_done"), sem("y_added")
        ln_var, ln_rstd, x1_done = sem("ln_var"), sem("ln_rstd"), sem("x1_done")
        dve_n, act_n, pool_n = sem("dve_n"), sem("act_n"), sem("pool_n")
        sp_passed, dve_passed = sem("sp_passed"), sem("dve_passed")
        NLOAD = 3

        block = ctx.enter_context(nc.Block())

        @block.sync
        def _(sp):
            loads = [(tab32[:, :], table32), (tab64[:, :], table64), (tab[:, 512:], table)]
            assert len(loads) == NLOAD
            for dst, src in loads:
                sp.dma_start(dst, src).then_inc(loaded, 16)

            def slot(at):
                a = Tile(at, 0)
                if a.static and a.live:
                    for dst, src in later.loads[a.t:a.t + 1]:
                        sp.dma_start(dst, src).then_inc(later.loaded, 16)
                if a.live:
                    a.free(sp, projected, 2)
                    carry(sp, sp_passed)
                    sp.dma_start(xTt[:, a.u2, :], xT[:, bass.ds(a.t * P, P)]).then_inc(a.ring(xT_in), 16)
                b = Tile(at, 1)
                if b.live:
                    b.wait(sp, v_copied)
                    carry(sp, sp_passed)
                    sp.dma_start(v_dram[bass.ds(b.t * P, P), :], vs[:, b.u2, :]).then_inc(b.ring(v_kept), 16)
                e = Tile(at, 5)
                if e.live:
                    e.wait_ring(sp, v_kept, 16)
                    carry(sp, sp_passed)
                    e.free(sp, summed, 4)
                    carry(sp, sp_passed)
                    for h in range(2):
                        sp.dma_start(VB[D * h:D * h + D, e.u4, :, D * h:D * h + D],
                                     v_dram[bass.ds(e.t * P, P), :].rearrange("(q t) d -> t q d", q=2)
                                     ).then_inc(e.ring(v_spread), 16)
                f = Tile(at, 7)
                if f.live:
                    f.free(sp, y_added, 2)
                    carry(sp, sp_passed)
                    sp.dma_start(xt[:, f.u2, :], x[bass.ds(f.t * P, P), :]).then_inc(f.ring(x_in), 16)
                g = Tile(at, 10)
                if g.live:
                    g.wait(sp, x1_done)
                    carry(sp, sp_passed)
                    sp.dma_start(x1[bass.ds(g.t * P, P), :], xo[:, g.u2, :]).then_inc(g.ring(stored), 16)
            pipeline(sp, slot, tiles, LAG + 1, U)
            for k in stored:
                sp.wait_ge(k, 16 * tiles // 2)

        @block.tensor
        def _(pe):
            pe.wait_ge(loaded, 16 * NLOAD)
            nc.tensor.matmul(ps_qT, wqcT[:, :], wqup[:, :], start=True, stop=True)
            for c in range(4):
                g, f = c // 2, (c % 2) * P
                last = nc.tensor.matmul(ps_mT[:, c * P:(c + 1) * P], wogT[:, g, f:f + P], wout[:, g, :],
                                        start=True, stop=True)
            last.then_inc(prods, 1)
            pe.wait_ge(weights, 1)
            pe.wait_ge(made, 1)

            def slot(at):
                a, d, e, h, k = (Tile(at, n) for n in (0, 3, 4, 7, 8))
                if h.live:
                    h.wait(pe, mixed)
                    h.free(pe, PT_copied, 1)
                    for c in range(4):
                        last = nc.tensor.transpose(
                            ps_PT[:, c * P:(c + 1) * P],
                            Pm[:, h.u2, 2 * c:2 * c + 2, :].rearrange("p h d -> p (h d)"), idf[:, :])
                    last.then_inc(P_turned, 1)
                if e.live:
                    e.wait(pe, qT_copied)
                    e.wait(pe, k_means)
                    e.free(pe, exped, 1)
                    for j in range(2):
                        nc.tensor.matmul(ps_S[:, j, :], idb[:, :], maskb[:, :], start=True, stop=False,
                                         skip_group_check=True)
                    for c in range(4):
                        for q in range(2):
                            last = nc.tensor.matmul(
                                ps_S[D * q:D * q + D, c // 2, (c % 2) * 2 * W:(c % 2 + 1) * 2 * W],
                                qT[:, e.u2, c, D * q:D * q + D],
                                KB[:, e.u2, q, :, :].rearrange("p h w -> p (h w)"),
                                start=False, stop=True, skip_group_check=True)
                    last.then_inc(scored, 1)
                if d.live:
                    d.wait(pe, roped)
                    d.wait(pe, k_normed)
                    d.free(pe, qT_copied, 1)
                    d.free(pe, kT_copied, 1)
                    for c in range(4):
                        nc.tensor.transpose(ps_qT[:, c * P:(c + 1) * P],
                                            qk[:, d.u4, 2 * c:2 * c + 2, :].rearrange("p h d -> p (h d)"), idf[:, :])
                    nc.tensor.transpose(ps_kT, kd[:, d.u2, :, :].rearrange("p h d -> p (h d)"),
                                        idf[:, :]).then_inc(turned, 1)
                if k.live:
                    k.wait(pe, mT_copied)
                    k.free(pe, y_added, 1)
                    before = Tile(at, 1)
                    if before.live:
                        before.wait(pe, squared)
                    for c in range(4):
                        last = nc.tensor.matmul(ps_y, mT[:, c, :], wc[:, c, :], start=(c == 0), stop=(c == 3))
                    last.then_inc(y_done, 1)
                if a.live:
                    a.wait_ring(pe, xT_in, 16)
                    a.free(pe, squared, 1)
                    if k.live:
                        k.wait(pe, y_added)
                    nc.tensor.matmul(flat[:, 0:512], xTt[:, a.u2, :], wqkv[:, 0:512], start=True, stop=True)
                    nc.tensor.matmul(flat[:, 512:640], xTt[:, a.u2, :], wqkv[:, 512:640],
                                     start=True, stop=True).then_inc(projected, 1)
                if h.live:
                    h.wait(pe, PT_copied)
                    h.wait_ring(pe, v_spread, 32)
                    h.free(pe, mT_copied, 1)
                    for q in range(2):
                        last = nc.tensor.matmul(
                            ps_mT.rearrange("p (c t) -> p c t", c=4)[:, :, D * q:D * q + D],
                            VB[:, h.u4, q, :], PT[:, :, D * q:D * q + D], start=True, stop=True)
                    last.then_inc(summed, 1)
            pipeline(pe, slot, tiles, LAG, U)

        @block.scalar
        def _(act):
            act.wait_ge(prods, 1)
            nc.scalar.activation(wqkv[:, 0:512], ps_qT, ACT.Copy).then_inc(act_n, 1)
            nc.scalar.activation(wc[:, :, :].rearrange("p c n -> p (c n)"), ps_mT, ACT.Copy).then_inc(act_n, 1)
            act.wait_ge(act_n, 2)
            act.sem_inc(weights, 1)

            def slot(at):
                a, d, e, h = (Tile(at, n) for n in (0, 3, 4, 7))
                if h.live:
                    h.wait(act, P_turned)
                    h.free(act, summed, 1)
                    nc.scalar.activation(PT[:, :, :].rearrange("p c t -> p (c t)"), ps_PT,
                                         ACT.Copy).then_inc(PT_copied, 1)
                if d.live:
                    d.wait(act, turned)
                    d.free(act, scored, 2)
                    nc.scalar.activation(qT[:, d.u2, :, :].rearrange("p c t -> p (c t)"), ps_qT,
                                         ACT.Copy).then_inc(qT_copied, 1)
                    for g in range(2):
                        last = nc.scalar.activation(KB[D * g:D * g + D, d.u2, :, g, 0:D],
                                                    ps_kT[D * g:D * g + D, :].rearrange("p (b k) -> p b k", b=2),
                                                    ACT.Copy)
                    last.then_inc(kT_copied, 1)
                if e.live:
                    e.wait(act, maxed)
                    e.free(act, mixed, 4)
                    for g in range(H):
                        last = nc.scalar.activation(E[:, e.u4, g, :], ps_Sh[:, g // 4, g % 4, 0:D], ACT.Exp,
                                                    bias=nb[:, e.u2, g:g + 1], scale=sc8[:, e.u4, g:g + 1],
                                                    accum_out=Z[:, e.u2, g:g + 1])
                    last.then_inc(exped, 1)
                    e.wait(act, args)
                    e.wait(act, gate_args)
                    nc.scalar.activation(ex[:, e.u2, :, :], arg[:, e.u2, :, :], ACT.Exp).then_inc(small_exp, 1)
                if a.live:
                    a.wait(act, projected)
                    a.free(act, turned, 4)
                    nc.scalar.activation(qk[:, a.u4, :, :], ps_qk, ACT.Copy).then_inc(kq_copied, 1)
                    a.wait_ring(act, v_kept, 16, back=2)
                    nc.scalar.activation(vs[:, a.u2, :], ps_v, ACT.Copy).then_inc(v_copied, 1)
                    a.free(act, mean_sq, 2)
                    nc.scalar.activation(sq[:, a.u2, :, :], ps_qk, ACT.Square).then_inc(squared, 1)
                if h.live:
                    h.wait(act, summed)
                    h.free(act, y_done, 1)
                    nc.scalar.activation(mT[:, :, :].rearrange("p c t -> p (c t)"), ps_mT,
                                         ACT.Copy).then_inc(mT_copied, 1)
            pipeline(act, slot, tiles, LAG, U)

        @block.gpsimd
        def _(pool):
            n = Count(pool, pool_n)
            G = nc.gpsimd
            n.add(G.memset(halfneg[:, :], -0.5))
            n.add(G.memset(root[:, :], D ** -0.5))
            G.memset(later.qz[:, :, :, :], 0.0).then_inc(later.cleared, 1)
            G.memset(later.VB[:, :, :, :, :], 0.0).then_inc(later.cleared, 1)
            G.memset(later.ones[:, :], 1.0).then_inc(later.cleared, 1)
            pool.wait_ge(later.cleared, 3)
            for g in range(2):
                G.memset(later.VB[T * g:T * g + T, :, :, :, 16 + g:17 + g], 1.0).then_inc(later.cleared, 1)
                pool.wait_ge(later.cleared, 4 + g)
            pool.wait_ge(loaded, 16 * NLOAD)
            n.add(G.tensor_scalar(nbg[:, :], bg[:, :], -1.0, None, ALU.mult))
            n.settle()

            def slot(at):
                b, e, f, k = (Tile(at, n) for n in (1, 4, 6, 8))
                if b.live:
                    b.wait(pool, kq_copied)
                    b.free(pool, roped, 1)
                    q = qk[:, b.u4, :, :]
                    G.tensor_tensor(tb[:, :, 0:16], q[:, :, 16:32],
                                    sin[:, 0:16].unsqueeze(1).to_broadcast([P, 9, 16]), ALU.mult)
                    G.tensor_tensor(tb[:, :, 16:32], q[:, :, 0:16],
                                    sin[:, 16:32].unsqueeze(1).to_broadcast([P, 9, 16]),
                                    ALU.mult).then_inc(sined, 1)
                if e.live:
                    e.wait(pool, scores_kept)
                    e.free(pool, small_exp, 2)
                    c = n.add(G.tensor_tensor(gl[:, :, :], s5[:, e.u2, :, 2:5],
                                              rinv[:, e.u4, 0:H].unsqueeze(2).to_broadcast([P, H, 3]), ALU.mult))
                    n.upto(c)
                    G.tensor_tensor(arg[:, e.u2, :, 4:7], nbg[:, :].unsqueeze(1).to_broadcast([P, H, 3]),
                                    gl[:, :, :], ALU.subtract).then_inc(gate_args, 1)
                if f.live:
                    f.wait(pool, mixing)
                    f.free(pool, P_turned, 2)
                    c = n.add(G.tensor_tensor(
                        Pm[:, f.u2, :, :], E[:, f.u4, :, :],
                        pa[:, f.u2, :].unsqueeze(2).to_broadcast([P, H, D]), ALU.mult))
                    n.upto(c)
                    Pv = Pm[:, f.u2, :, :].rearrange("p h (n k) -> p (h n) k", n=2)
                    G.tensor_tensor(
                        Pv, Pv, pc[:, f.u2, :, :].rearrange("p h n -> p (h n)").unsqueeze(2)
                        .to_broadcast([P, 2 * H, 32]), ALU.add).then_inc(mixed, 1)
                if k.live:
                    k.wait(pool, ln_var)
                    G.tensor_tensor(rs[:, k.u2, :], ve[:, k.u2, :], halfneg[:, 0:1], ALU.pow).then_inc(ln_rstd, 1)
                if b.live:
                    b.wait(pool, mean_sq)
                    b.free(pool, exped, 4)
                    G.tensor_tensor(rinv[:, b.u4, :], ms[:, b.u2, :], halfneg[:, 0:9], ALU.pow).then_inc(inv_rms, 1)
                    b.wait(pool, inv_rms)
                    G.tensor_tensor(sc8[:, b.u4, :], rinv[:, b.u4, 0:H], root[:, :], ALU.mult).then_inc(scales, 1)
            pipeline(pool, slot, tiles, LAG, U, [n])

        @block.vector
        def _(dve):
            n = Count(dve, dve_n)
            V = nc.vector
            n.add(V.memset(VB[:, :, :, :], 0.0))
            n.add(V.memset(KB[:, :, :, :, :], 0.0))
            dve.wait_ge(loaded, 16 * NLOAD)
            n.add(V.tensor_copy(idb[:, :], idf[:, :]))
            n.add(V.tensor_copy(maskb[:, :], maskf[:, :]))
            for h in range(2):
                n.add(V.tensor_tensor(gg[:, h, :], gq[:, :], gk[:, :], ALU.mult))
            n.add(V.tensor_scalar(wg[:, :], wgate[:, :], gqc[:, 0:1], None, ALU.mult))
            n.settle()
            for h in range(2):
                for i in range(2):
                    for q in range(2):
                        n.add(V.tensor_copy(KB[D * h:D * h + D, i, q, h, 66:69], wg[D * h:D * h + D, :]))
            n.settle()
            dve.sem_inc(made, 1)

            def slot(at):
                b, c, d, e, f, k, l = (Tile(at, m) for m in (1, 2, 3, 4, 5, 8, 9))
                if l.live:
                    l.wait(dve, ln_rstd)
                    l.wait_ring(dve, stored, 16, back=2)
                    V.tensor_scalar(xo[:, l.u2, :], r[:, l.u2, :], mv[:, l.u2, 0:1], rs[:, l.u2, 0:1],
                                    ALU.subtract, ALU.mult).then_inc(x1_done, 1)
                if e.live:
                    e.wait(dve, scored)
                    n_max = n.add(V.tensor_reduce(mx[:, :].rearrange("p (a h) -> p a h", a=2),
                                                  ps_Sh[:, :, :, 0:D], AX.X, ALU.max))
                    e.free(dve, gate_args, 2)
                    V.tensor_copy(s5[:, e.u2, :, :].rearrange("p (a h) w -> p a h w", a=2),
                                  ps_Sh[:, :, :, D:W]).then_inc(scores_kept, 1)
                    n.upto(n_max)
                    e.wait(dve, scales)
                    e.free(dve, exped, 2)
                    V.scalar_tensor_tensor(nb[:, e.u2, :], mx[:, :], -1.0, sc8[:, e.u4, :], ALU.mult,
                                           ALU.mult).then_inc(maxed, 1)
                if b.live:
                    b.wait(dve, kq_copied)
                    q = qk[:, b.u4, :, :]
                    n_ta = n.add(V.tensor_tensor(ta[:, :, :], q[:, :, 0:32],
                                                 cos[:, :].unsqueeze(1).to_broadcast([P, 9, 32]), ALU.mult))
                if e.live:
                    e.wait(dve, scores_kept)
                    n_un = n.add(V.scalar_tensor_tensor(
                        un[:, :, :], s5[:, e.u2, :, 0:2], 1.0 / 32,
                        sc8[:, e.u4, :].unsqueeze(2).to_broadcast([P, H, 2]), ALU.mult, ALU.mult))
                if k.live:
                    k.wait(dve, y_done)
                    k.wait_ring(dve, x_in, 16)
                    V.tensor_tensor(r[:, k.u2, :], ps_y, xt[:, k.u2, :], ALU.add).then_inc(y_added, 1)
                if e.live:
                    n.upto(n_un)
                    n_mc = n.add(V.tensor_tensor(mc[:, :], un[:, :, 0], un[:, :, 1], ALU.max))
                    e.wait(dve, maxed)
                    e.free(dve, small_exp, 2)
                    n.add(V.tensor_tensor(arg[:, e.u2, :, 3], snk[:, :], nb[:, e.u2, :], ALU.add))
                if k.live:
                    k.wait(dve, y_added)
                    n_bn = n.add(V.bn_stats(st[:, :], r[:, k.u2, :]))
                if e.live:
                    n.upto(n_mc)
                    n_mc = n.add(V.tensor_tensor(mc[:, :], mc[:, :], snk[:, :], ALU.max))
                if b.live:
                    n.upto(n_ta)
                    b.wait(dve, sined)
                    V.tensor_tensor(q[:, :, 0:32], ta[:, :, :], tb[:, :, :], ALU.add).then_inc(roped, 1)
                if e.live:
                    n.upto(n_mc)
                    n.add(V.tensor_tensor(arg[:, e.u2, :, 0:2], un[:, :, :],
                                          mc[:, :].unsqueeze(2).to_broadcast([P, H, 2]), ALU.subtract))
                    n_arg = n.add(V.tensor_tensor(arg[:, e.u2, :, 2], snk[:, :], mc[:, :], ALU.subtract))
                if k.live:
                    n.upto(n_bn)
                    carry(dve, dve_passed)
                    n_mv = n.add(V.bn_aggr(mv[:, k.u2, :], st[:, :]))
                if e.live:
                    n.upto(n_arg)
                    dve.sem_inc(args, 1)
                if d.live:
                    d.wait(dve, kT_copied)
                    V.tensor_reduce(KB[:, d.u2, :, :, 64:66],
                                    KB[:, d.u2, :, :, 0:D].rearrange("p b h (n k) -> p (b h) n k", n=2),
                                    AX.X, ALU.add).then_inc(k_means, 1)
                if c.live:
                    c.wait(dve, inv_rms)
                    c.wait(dve, roped)
                    c.free(dve, turned, 2)
                    V.scalar_tensor_tensor(kd[:, c.u2, :, :], qk[:, c.u4, 8:9, :].to_broadcast([P, 2, D]),
                                           rinv[:, c.u4, 8:9], gg[:, :, :], ALU.mult,
                                           ALU.mult).then_inc(k_normed, 1)
                if k.live:
                    n.upto(n_mv)
                    V.tensor_scalar(ve[:, k.u2, :], mv[:, k.u2, 1:2], 1e-5, None, ALU.add).then_inc(ln_var, 1)
                if f.live:
                    f.wait(dve, small_exp)
                    n.add(V.tensor_reduce(den[:, :, 2], ex[:, f.u2, :, 0:3], AX.X, ALU.add))
                    n.add(V.tensor_scalar(den[:, :, 3:6], ex[:, f.u2, :, 4:7], 1.0, None, ALU.add))
                    n.add(V.tensor_copy(den[:, :, 0], Z[:, f.u2, :]))
                    n_den = n.add(V.tensor_tensor(den[:, :, 1], Z[:, f.u2, :], ex[:, f.u2, :, 3], ALU.add))
                if b.live:
                    b.wait(dve, squared)
                    n_ss = n.add(V.tensor_reduce(ss[:, :], sq[:, b.u2, :, :], AX.X, ALU.add))
                if f.live:
                    n.upto(n_den)
                    n_rd = n.add(V.reciprocal(rd[:, :, :], den[:, :, :]))
                if b.live:
                    n.upto(n_ss)
                    b.free(dve, inv_rms, 2)
                    V.tensor_scalar(ms[:, b.u2, :], ss[:, :], 1.0 / D, 1e-6, ALU.mult, ALU.add).then_inc(mean_sq, 1)
                if f.live:
                    n.upto(n_rd)
                    n_gs = n.add(V.tensor_reduce(gs[:, :], rd[:, :, 3:6], AX.X, ALU.add))
                    n.add(V.tensor_tensor(a1[:, :], rd[:, :, 4], rd[:, :, 0], ALU.mult))
                    n_a2 = n.add(V.tensor_tensor(a2[:, :], rd[:, :, 5], rd[:, :, 1], ALU.mult))
                    n.upto(n_gs)
                    n_gs = n.add(V.tensor_scalar(gs[:, :], gs[:, :], 1e-6, None, ALU.max))
                    n.add(V.tensor_tensor(a3[:, :], rd[:, :, 2], rd[:, :, 3], ALU.mult))
                    n.upto(n_a2)
                    n.add(V.tensor_tensor(a1[:, :], a1[:, :], a2[:, :], ALU.add))
                    n.upto(n_gs)
                    n_rg = n.add(V.reciprocal(rg[:, :], gs[:, :]))
                if f.live:
                    n.upto(n_rg)
                    f.free(dve, mixed, 2)
                    n.add(V.tensor_tensor(pa[:, f.u2, :], a1[:, :], rg[:, :], ALU.mult))
                    n.add(V.tensor_tensor(a3[:, :], a3[:, :], rg[:, :], ALU.mult))
                    n.settle()
                    V.scalar_tensor_tensor(pc[:, f.u2, :, :], ex[:, f.u2, :, 0:2], 1.0 / 32,
                                           a3[:, :].unsqueeze(2).to_broadcast([P, H, 2]),
                                           ALU.mult, ALU.mult).then_inc(mixing, 1)
            pipeline(dve, slot, tiles, LAG, U, [n])


class Later:

    WIDTH = 5 * P + 4 + 4 + 3 * 8 + 8 * 4 + 8 * 2 * P

    def __init__(self, nc, ctx, ap):
        E, I = 8, 256

        def sb(name, shape, dt=F32):
            return ctx.enter_context(nc.sbuf_tensor("l_" + name, shape, dt))

        self.table = sb("table", [P, self.WIDTH])
        (self.idf, self.wq, self.wk, self.wv, self.wo, self.hm, self.bqc, self.bkc, self.bvc, self.ns, self.gw, self.gb,
         self.rt, b1, w2) = columns(self.table[:, :], P, P, P, P, P, 4, 1, 1, 1, 1, E, E, E, E * 4, E * 2 * P)
        self.bor = sb("bor", [1, P])
        self.ones = sb("ones", [1, P])
        self.qz = sb("qz", [P, 4, 4, P])
        self.VB = sb("VB", [P, 4, 2, 8, 64])
        self.W1 = sb("W1", [P, E, 2, I])
        self.W1h = sb("W1h", [P, E, 2, I], F32R)
        self.W1l = sb("W1l", [P, E, 2, I], F32R)
        self.B1 = b1.rearrange("p (e h j) -> p e h j", e=E, h=2)
        self.W2 = w2.rearrange("p (e j n) -> p e j n", e=E, j=2)
        self.B2 = sb("B2", [E, P])
        self.loaded = ctx.enter_context(nc.semaphore("l_loaded"))
        self.cleared = ctx.enter_context(nc.semaphore("l_cleared"))
        self.W1_split = ctx.enter_context(nc.semaphore("l_W1_split"))
        self.loads = [(self.table[:, :], ap["later_table"]), (self.W1[:, :, :, :], ap["w1"]), (self.B2[:, :], ap["b2"]),
                      (self.bor[:, :], ap["bo"].rearrange("(a d) -> a d", a=1))]
        self.all_loaded = 16 * len(self.loads)


def cross_attention(nc, x1, ctxT, x2, tiles, later):
    H, D, T = 16, 8, 64
    LAG, U = 9, 4
    with ExitStack() as ctx:
        def sb(name, shape, dt=F32):
            return ctx.enter_context(nc.sbuf_tensor("x_" + name, shape, dt))

        def sem(name):
            return ctx.enter_context(nc.semaphore("x_" + name))

        wq, wk, wv, wo, idf, hm = later.wq, later.wk, later.wv, later.wo, later.idf, later.hm
        bqc, bkc, bvc, bor = later.bqc, later.bkc, later.bvc, later.bor
        ones, qz, VB = later.ones, later.qz, later.VB
        borow = sb("borow", [1, P])
        W1c = sb("W1c", [P, 8, 2, 256])
        bob = sb("bob", [P, P])
        halfneg = sb("halfneg", [P, 1])
        xa = sb("xa", [P, 2, P])
        ct = sb("ct", [P, 4, P])
        x1T = sb("x1T", [P, 2, P])
        kT = sb("kT", [P, 2, P])
        KB = sb("KB", [P, 2, 2, 4, T])
        mx = sb("mx", [P, H])
        sh = sb("sh", [P, 2, H, T])
        E = sb("E", [P, 2, H, T])
        PT = sb("PT", [P, 8, P])
        rz = sb("rz", [P, H])
        o = sb("o", [P, 2, P])
        oT = sb("oT", [P, 2, P])
        xb = sb("xb", [P, 2, P])
        xr = sb("xr", [P, 2, P])
        r = sb("r", [P, 2, P])
        st = sb("st", [P, 6])
        mv = sb("mv", [P, 2, 2])
        ve = sb("ve", [P, 2, 1])
        rs = sb("rs", [P, 2, 1])
        xo = sb("xo", [P, 2, P])

        ps = ctx.enter_context(nc.psum_tensor("x_ps", [P, 8, 512], F32))
        ps_x, ps_y, ps_oT = ps[:, 0, 0:P], ps[:, 0, P:2 * P], ps[:, 0, 2 * P:3 * P]
        ps_q, ps_k = ps[:, 1, 0:P], ps[:, 1, P:2 * P]
        ps_v = ps[:, 2, 0:2 * P].rearrange("p (b f) -> p b f", b=2)
        ps_S = ps[:, 3:5, :].rearrange("p a (h k) -> p (a h) k", k=T)
        ps_PT = ps[:, 5:7, :].rearrange("p a (c t) -> p (a c) t", t=P)
        ps_O = ps[:, 7, :].rearrange("p (c n) -> p c n", n=64)

        bias_sum, bias_row, bias_all = (sem(n) for n in ("bias_sum", "bias_row", "bias_all"))
        bias_done, W1_cut = sem("bias_done"), sem("W1_cut")
        xa_in, xb_in, stored = ([sem(f"{k}{i}") for i in range(2)] for k in ("xa_in", "xb_in", "stored"))
        ct_in = [sem(f"ct_in{i}") for i in range(4)]
        x_turned, x1T_ready, projected, q_ready, k_ready, v_ready = (
            sem(n) for n in ("x_turned", "x1T_ready", "projected", "q_ready", "k_ready", "v_ready"))
        k_spread, scored, shifted, exped = sem("k_spread"), sem("scored"), sem("shifted"), sem("exped")
        P_turned, PT_ready, summed, normed = sem("P_turned"), sem("PT_ready"), sem("summed"), sem("normed")
        o_turned, oT_ready, y_done, residual, y_added = (
            sem(n) for n in ("o_turned", "oT_ready", "y_done", "residual", "y_added"))
        ln_var, ln_rstd, x2_done = sem("ln_var"), sem("ln_rstd"), sem("x2_done")
        dve_n, pool_n = sem("dve_n"), sem("pool_n")
        sp_passed, dve_passed = sem("sp_passed"), sem("dve_passed")
        block = ctx.enter_context(nc.Block())

        @block.sync
        def _(sp):
            def slot(at):
                a, h, l = (Tile(at, n) for n in (0, 7, 10))
                if a.live:
                    a.free(sp, x_turned, 2)
                    carry(sp, sp_passed)
                    sp.dma_start(xa[:, a.u2, :], x1[bass.ds(a.t * P, P), :]).then_inc(a.ring(xa_in), 16)
                    a.free(sp, projected, 4)
                    carry(sp, sp_passed)
                    sp.dma_start(ct[:, a.u4, :], ctxT[:, bass.ds(a.t * P, P)]).then_inc(a.ring(ct_in), 16)
                if h.live:
                    h.free(sp, residual, 2)
                    carry(sp, sp_passed)
                    sp.dma_start(xb[:, h.u2, :], x1[bass.ds(h.t * P, P), :]).then_inc(h.ring(xb_in), 16)
                if l.live:
                    l.wait(sp, x2_done)
                    carry(sp, sp_passed)
                    sp.dma_start(x2[bass.ds(l.t * P, P), :], xo[:, l.u2, :]).then_inc(l.ring(stored), 16)
            pipeline(sp, slot, tiles, LAG + 1, U)
            for k in stored:
                sp.wait_ge(k, 16 * tiles // 2)

        @block.tensor
        def _(pe):
            pe.wait_ge(later.loaded, later.all_loaded)
            pe.wait_ge(later.cleared, 5)
            nc.tensor.matmul(ps_x[0:1, :], bvc[:, :], wo[:, :], start=True, stop=True).then_inc(bias_sum, 1)
            pe.wait_ge(bias_row, 1)
            nc.tensor.matmul(ps_q, ones[:, :], borow[:, :], start=True, stop=True).then_inc(bias_all, 1)
            pe.wait_ge(bias_done, 1)

            def slot(at):
                a, b, d, f, h, k = (Tile(at, n) for n in (0, 1, 3, 5, 7, 8))
                if k.live:
                    k.wait(pe, oT_ready)
                    k.free(pe, y_added, 1)
                    before = Tile(at, 1)
                    if before.live:
                        before.wait(pe, x1T_ready)
                    nc.tensor.matmul(ps_y, oT[:, k.u2, :], wo[:, :], start=True, stop=True).then_inc(y_done, 1)
                if f.live:
                    f.wait(pe, exped)
                    f.free(pe, PT_ready, 1)
                    for c in range(8):
                        last = nc.tensor.transpose(ps_PT[:, c, :],
                                                   E[:, f.u2, 2 * c:2 * c + 2, :].rearrange("p h k -> p (h k)"),
                                                   idf[:, :])
                    last.then_inc(P_turned, 1)
                if d.live:
                    d.wait(pe, q_ready)
                    d.wait(pe, k_spread)
                    d.free(pe, shifted, 1)
                    for g in range(4):
                        for q in range(2):
                            last = nc.tensor.matmul(
                                ps_S[T * q:T * q + T, 4 * g:4 * g + 4, :].rearrange("p h k -> p (h k)"),
                                qz[:, d.u4, g, T * q:T * q + T],
                                KB[:, d.u2, q, :, :].rearrange("p h k -> p (h k)"), start=True, stop=True)
                    last.then_inc(scored, 1)
                if a.live:
                    a.wait_ring(pe, xa_in, 16)
                    a.free(pe, x1T_ready, 1)
                if h.live:
                    h.wait(pe, normed)
                    h.free(pe, oT_ready, 1)
                if k.live:
                    k.wait(pe, y_added)
                if a.live:
                    nc.tensor.transpose(ps_x, xa[:, a.u2, :], idf[:, :]).then_inc(x_turned, 1)
                if h.live:
                    nc.tensor.transpose(ps_oT, o[:, h.u2, :], idf[:, :]).then_inc(o_turned, 1)
                if b.live:
                    b.wait(pe, x1T_ready)
                    b.wait_ring(pe, ct_in, 16)
                    b.free(pe, q_ready, 1)
                    b.free(pe, k_ready, 1)
                    b.free(pe, v_ready, 1)
                    nc.tensor.matmul(ps_q, wq[:, :], x1T[:, b.u2, :], start=True, stop=True)
                    nc.tensor.matmul(ps_k, wk[:, :], ct[:, b.u4, :], start=True, stop=True)
                    for q in range(2):
                        for g in range(2):
                            last = nc.tensor.matmul(ps_v[T * g:T * g + T, q, :], ct[:, b.u4, T * q:T * q + T],
                                                    wv[:, :], start=True, stop=True)
                    last.then_inc(projected, 1)
                if f.live:
                    f.wait(pe, PT_ready)
                    f.wait(pe, v_ready)
                    f.free(pe, normed, 1)
                    for c in range(8):
                        for q in range(2):
                            last = nc.tensor.matmul(ps_O[T * q:T * q + T, c, :], PT[:, c, T * q:T * q + T],
                                                    VB[:, f.u4, q, c, :], start=True, stop=True)
                    last.then_inc(summed, 1)
            pipeline(pe, slot, tiles, LAG, U)

        @block.scalar
        def _(act):
            def slot(at):
                a, b, e, f, h = (Tile(at, n) for n in (0, 1, 4, 5, 7))
                if e.live:
                    e.wait(act, shifted)
                    e.free(act, P_turned, 2)
                    nc.scalar.activation(E[:, e.u2, :, :], sh[:, e.u2, :, :], ACT.Exp,
                                         scale=D ** -0.5).then_inc(exped, 1)
                if f.live:
                    f.wait(act, P_turned)
                    f.free(act, summed, 1)
                    nc.scalar.activation(PT[:, :, :], ps_PT, ACT.Copy).then_inc(PT_ready, 1)
                if a.live:
                    a.wait(act, x_turned)
                    if h.live:
                        h.wait(act, o_turned)
                    a.free(act, projected, 2)
                    nc.scalar.activation(x1T[:, a.u2, :], ps_x, ACT.Copy).then_inc(x1T_ready, 1)
                if h.live:
                    h.wait(act, o_turned)
                    h.free(act, y_done, 2)
                    nc.scalar.activation(oT[:, h.u2, :], ps_oT, ACT.Copy).then_inc(oT_ready, 1)
                if b.live:
                    b.wait(act, projected)
                    b.free(act, scored, 4)
                    for g in range(4):
                        s = slice(32 * g, 32 * g + 32)
                        last = nc.scalar.activation(qz[s, b.u4, g, :], ps_q[s, :], ACT.Identity, bias=bqc[s, :])
                    last.then_inc(q_ready, 1)
                    b.free(act, k_spread, 2)
                    nc.scalar.activation(kT[:, b.u2, :], ps_k, ACT.Identity, bias=bkc[:, :]).then_inc(k_ready, 1)
                    b.free(act, summed, 4)
                    for g in range(2):
                        s = slice(T * g, T * g + T)
                        last = nc.scalar.activation(
                            VB[s, b.u4, :, :, D * g:D * g + D],
                            ps_v[s, :, :].rearrange("p b (c d) -> p b c d", d=2 * D)[:, :, :, D * g:D * g + D],
                            ACT.Copy)
                    last.then_inc(v_ready, 1)
            act.wait_ge(later.loaded, later.all_loaded)
            act.wait_ge(later.cleared, 5)
            pipeline(act, slot, tiles, LAG, U)

        @block.gpsimd
        def _(pool):
            nc.gpsimd.memset(halfneg[:, :], -0.5).then_inc(pool_n, 1)
            pool.wait_ge(pool_n, 1)
            pool.wait_ge(bias_done, 1)
            pool.wait_ge(W1_cut, 1)
            nc.gpsimd.tensor_copy(later.W1h[:, :, :, :], W1c[:, :, :, :]).then_inc(later.W1_split, 1)
            nc.gpsimd.tensor_tensor(later.W1l[:, :, :, :], later.W1[:, :, :, :], W1c[:, :, :, :],
                                    ALU.subtract).then_inc(later.W1_split, 1)

            def slot(at):
                h, k = Tile(at, 7), Tile(at, 8)
                if k.live:
                    k.wait(pool, ln_var)
                    nc.gpsimd.tensor_tensor(rs[:, k.u2, :], ve[:, k.u2, :], halfneg[:, :],
                                            ALU.pow).then_inc(ln_rstd, 1)
                if h.live:
                    h.wait_ring(pool, xb_in, 16)
                    h.free(pool, y_added, 2)
                    nc.gpsimd.tensor_tensor(xr[:, h.u2, :], xb[:, h.u2, :], bob[:, :], ALU.add).then_inc(residual, 1)
            pipeline(pool, slot, tiles, LAG, U)

        @block.vector
        def _(dve):
            n = Count(dve, dve_n)
            V = nc.vector
            dve.wait_ge(later.loaded, later.all_loaded)
            dve.wait_ge(bias_sum, 1)
            V.tensor_tensor(borow[:, :], ps_x[0:1, :], bor[:, :], ALU.add).then_inc(bias_row, 1)
            dve.wait_ge(bias_all, 1)
            V.tensor_copy(bob[:, :], ps_q).then_inc(bias_done, 1)
            V.tensor_scalar(W1c[:, :, :, :].bitcast(U32), later.W1[:, :, :, :].bitcast(U32), HIGH, None,
                            ALU.bitwise_and).then_inc(W1_cut, 1)

            def slot(at):
                c, d, g, k, l = (Tile(at, m) for m in (2, 3, 6, 8, 9))
                if l.live:
                    l.wait(dve, ln_rstd)
                    l.wait_ring(dve, stored, 16, back=2)
                    V.tensor_scalar(xo[:, l.u2, :], r[:, l.u2, :], mv[:, l.u2, 0:1], rs[:, l.u2, 0:1],
                                    ALU.subtract, ALU.mult).then_inc(x2_done, 1)
                if g.live:
                    g.wait(dve, summed)
                    n_rz = n.add(V.reciprocal(rz[:, :].rearrange("p (c h) -> p c h", h=2), ps_O[:, :, 16:18]))
                if k.live:
                    k.wait(dve, y_done)
                    k.wait(dve, residual)
                    V.tensor_tensor(r[:, k.u2, :], ps_y, xr[:, k.u2, :], ALU.add).then_inc(y_added, 1)
                if g.live:
                    n.upto(n_rz)
                    g.free(dve, o_turned, 2)
                    V.tensor_tensor(o[:, g.u2, :].rearrange("p (h d) -> p h d", d=D).rearrange("p (c h) d -> p c h d", h=2),
                                    ps_O[:, :, 0:16].rearrange("p c (h d) -> p c h d", d=D),
                                    rz[:, :].rearrange("p (c h) -> p c h", h=2).unsqueeze(3).to_broadcast([P, 8, 2, D]),
                                    ALU.mult).then_inc(normed, 1)
                if d.live:
                    d.wait(dve, scored)
                    n_mx = n.add(V.tensor_reduce(mx[:, :], ps_S, AX.X, ALU.max))
                if k.live:
                    k.wait(dve, y_added)
                    n_st = n.add(V.bn_stats(st[:, :], r[:, k.u2, :]))
                if d.live:
                    n.upto(n_mx)
                    d.free(dve, exped, 2)
                    V.tensor_tensor(sh[:, d.u2, :, :], ps_S, mx[:, :].unsqueeze(2).to_broadcast([P, H, T]),
                                    ALU.subtract).then_inc(shifted, 1)
                if k.live:
                    n.upto(n_st)
                    carry(dve, dve_passed)
                    n_mv = n.add(V.bn_aggr(mv[:, k.u2, :], st[:, :]))
                if c.live:
                    c.wait(dve, k_ready)
                    c.free(dve, scored, 2)
                    V.tensor_tensor(KB[:, c.u2, :, :, :],
                                    kT[:, c.u2, :].rearrange("p (b k) -> p b k", b=2).unsqueeze(2).to_broadcast([P, 2, 4, T]),
                                    hm[:, :].unsqueeze(1).unsqueeze(3).to_broadcast([P, 2, 4, T]),
                                    ALU.mult).then_inc(k_spread, 1)
                if k.live:
                    n.upto(n_mv)
                    V.tensor_scalar(ve[:, k.u2, :], mv[:, k.u2, 1:2], 1e-5, None, ALU.add).then_inc(ln_var, 1)
            pipeline(dve, slot, tiles, LAG, U, [n])

def experts(nc, x2, out, tiles, later):
    E, I, K = 8, 256, 2
    LAG, U = 2, 2
    N = K * P
    units = tiles // K
    with ExitStack() as ctx:
        def sb(name, shape, dt=F32):
            return ctx.enter_context(nc.sbuf_tensor("m_" + name, shape, dt))

        def sem(name):
            return ctx.enter_context(nc.semaphore("m_" + name))

        W1h, W1l, B1, W2, B2 = later.W1h, later.W1l, later.B1, later.W2, later.B2
        ns, gw, gb, rt, idf = later.ns, later.gw, later.gb, later.rt, later.idf
        B1g = sb("B1g", [P, E, 2])
        B1l = sb("B1l", [P, E, 2])
        s7 = sb("s7", [P, 1])
        halfneg = sb("halfneg", [P, K])
        x = sb("x", [P, 2, K, P])
        sq = sb("sq", [P, K, P])
        ss = sb("ss", [P, 2, K])
        ms = sb("ms", [P, K])
        rr = sb("rr", [P, 2, K])
        t = sb("t", [P, K, P])
        tT = sb("tT", [P, 2, N])
        tTc = sb("tTc", [P, N])
        tTh = sb("tTh", [P, 2, N], F32R)
        tTl = sb("tTl", [P, 2, N], F32R)
        lg = sb("lg", [P, K, E])
        m1, m2, r1, r2, df = (sb(n_, [P, K]) for n_ in ("m1", "m2", "r1", "r2", "df"))
        eq, oh1, oh2, l2 = (sb(n_, [P, K, E]) for n_ in ("eq", "oh1", "oh2", "l2"))
        p1 = sb("p1", [P, K])
        p2 = sb("p2", [P, K])
        we = sb("we", [P, 2, K, E])
        wT = sb("wT", [E, K, P])
        acc = sb("acc", [P, 2, K, P])
        xg = sb("xg", [P, E, 2, N])
        xl = sb("xl", [P, E, 2, N])
        sg = sb("sg", [P, 4, 2, N])
        pr = sb("pr", [P, 4, 2, N])
        h = sb("h", [P, E, 2, N])
        st = sb("st", [P, K, 6])
        mv = sb("mv", [P, 2, K, 2])
        ve = sb("ve", [P, 2, K])
        rs = sb("rs", [P, 2, K])
        xo = sb("xo", [P, 2, K, P])

        ps = ctx.enter_context(nc.psum_tensor("m_ps", [P, 8, 512], F32))
        ps_g = ps[:, 0:2, :].rearrange("p a (j n) -> p a j n", j=2)
        ps_l = ps[:, 2:4, :].rearrange("p a (j n) -> p a j n", j=2)
        ps_y = ps[:, 4:6, 0:N].rearrange("p a (k n) -> p a k n", k=K)
        ps_t = ps[:, 6, 0:N]
        ps_lg = ps[:, 7, 0:K * E].rearrange("p (k e) -> p k e", e=E)
        ps_wT = ps[0:E, 6, N:2 * N].rearrange("p (k n) -> p k n", k=K)
        ps_b = ps[:, 7, N:2 * N].rearrange("p (k n) -> p k n", k=K)

        made, tT_split = sem("made"), sem("tT_split")
        x_in, stored = ([sem(f"{k}{i}") for i in range(2)] for k in ("x_in", "stored"))
        squared, mean_sq, inv_rms, normed, t_turned, tT_ready = (
            sem(k) for k in ("squared", "mean_sq", "inv_rms", "normed", "t_turned", "tT_ready"))
        logits, logit_gap, shares, routed, w_turned, wT_ready, biased, acc_ready = (
            sem(k) for k in ("logits", "logit_gap", "shares", "routed", "w_turned", "wT_ready", "biased", "acc_ready"))
        up, glu_ready, lin_ready, clipped, gated, prod_ready, act_ready, down, added = (
            sem(k) for k in ("up", "glu_ready", "lin_ready", "clipped", "gated", "prod_ready", "act_ready", "down", "added"))
        ln_var, ln_rstd, out_done = sem("ln_var"), sem("ln_rstd"), sem("out_done")
        dve_n, pool_n = sem("dve_n"), sem("pool_n")
        sp_passed, dve_passed = sem("sp_passed"), sem("dve_passed")

        def step(eng, tile, sem_, e, back=0):
            if not tile.static or tile.t * E + e >= back:
                eng.wait_ge(sem_, tile.t * E + (e + 1 - back))

        def product(dst, w_high, w_low, t_high, t_low):
            nc.tensor.matmul(dst, w_high, t_high, start=True, stop=False)
            nc.tensor.matmul(dst, w_high, t_low, start=False, stop=False)
            return nc.tensor.matmul(dst, w_low, t_high, start=False, stop=True)

        block = ctx.enter_context(nc.Block())

        @block.sync
        def _(sp):
            def slot(at):
                a, d = Tile(at, 0), Tile(at, 3)
                if a.live:
                    a.free(sp, acc_ready, 2)
                    carry(sp, sp_passed)
                    sp.dma_start(x[:, a.u2, :, :], x2[bass.ds(a.t * N, N), :].rearrange("(k p) d -> p k d", p=P))\
                        .then_inc(a.ring(x_in), 16)
                if d.live:
                    d.wait(sp, out_done)
                    carry(sp, sp_passed)
                    sp.dma_start(out[bass.ds(d.t * N, N), :].rearrange("(k p) d -> p k d", p=P), xo[:, d.u2, :, :])\
                        .then_inc(d.ring(stored), 16)
            pipeline(sp, slot, units, LAG + 1, U)
            for k in stored:
                sp.wait_ge(k, 16 * units // 2)

        @block.tensor
        def _(pe):
            pe.wait_ge(later.loaded, later.all_loaded)
            pe.wait_ge(later.W1_split, 2)

            def slot(at):
                a, b, c = (Tile(at, n_) for n_ in (0, 1, 2))
                for e in range(E):
                    if b.live:
                        if e == 0:
                            b.wait(pe, tT_split, 2)
                        step(pe, b, glu_ready, e, 2)
                        step(pe, b, lin_ready, e, 2)
                        for half, ps_up in ((0, ps_g), (1, ps_l)):
                            for j in range(2):
                                last = product(ps_up[:, e % 2, j, :], W1h[:, e, half, j * P:(j + 1) * P],
                                               W1l[:, e, half, j * P:(j + 1) * P], tTh[:, b.u2, :], tTl[:, b.u2, :])
                        last.then_inc(up, 1)
                    if a.live and e == 3:
                        a.wait(pe, normed)
                        a.free(pe, wT_ready, 1)
                        a.free(pe, tT_ready, 1)
                        for k in range(K):
                            last = nc.tensor.transpose(ps_t[:, k * P:(k + 1) * P], t[:, k, :], idf[:, :])
                        last.then_inc(t_turned, 1)
                    if a.live and e == 5:
                        a.wait(pe, tT_ready)
                        a.free(pe, acc_ready, 1)
                        for k in range(K):
                            last = nc.tensor.matmul(ps_lg[:, k, :], tT[:, a.u2, k * P:(k + 1) * P], gw[:, :],
                                                    start=True, stop=True)
                        last.then_inc(logits, 1)
                    if b.live and e == 2:
                        b.wait(pe, routed)
                        for k in range(K):
                            last = nc.tensor.transpose(ps_wT[:, k, :], we[:, b.u2, k, :], idf[:, :])
                        last.then_inc(w_turned, 1)
                    if b.live and e == 3:
                        b.wait(pe, wT_ready)
                        for k in range(K):
                            last = nc.tensor.matmul(ps_b[:, k, :], wT[:, k, :], B2[:, :], start=True, stop=True)
                        last.then_inc(biased, 1)
                    o, oe = (b, e - 4) if e >= 4 else (c, e + 4)
                    if o.live:
                        step(pe, o, act_ready, oe)
                        step(pe, o, added, oe, 2)
                        for k in range(K):
                            for j in range(2):
                                last = nc.tensor.matmul(ps_y[:, oe % 2, k, :], h[:, oe, j, k * P:(k + 1) * P],
                                                        W2[:, oe, j, :], start=(j == 0), stop=(j == 1))
                        last.then_inc(down, 1)
            pipeline(pe, slot, units, LAG, U)

        @block.scalar
        def _(act):
            act.wait_ge(made, 3)

            def slot(at):
                a, b = Tile(at, 0), Tile(at, 1)
                for e in range(E):
                    if a.live and e == 0:
                        a.wait_ring(act, x_in, 16)
                        a.free(act, mean_sq, 2)
                        for k in range(K):
                            last = nc.scalar.activation(sq[:, k, :], x[:, a.u2, k, :], ACT.Square,
                                                        accum_out=ss[:, a.u2, k:k + 1])
                        last.then_inc(squared, 1)
                    if a.live and e == 4:
                        a.wait(act, t_turned)
                        a.free(act, tT_split, 2, 2)
                        a.free(act, logits, 2)
                        nc.scalar.activation(tT[:, a.u2, :], ps_t, ACT.Copy, scale=ns[:, :]).then_inc(tT_ready, 1)
                    if b.live:
                        step(act, b, up, e)
                        step(act, b, prod_ready, e, E)
                        for j in range(2):
                            last = nc.scalar.activation(xg[:, e, j, :], ps_g[:, e % 2, j, :], ACT.Relu,
                                                        bias=B1g[:, e, j:j + 1], scale=-1.0)
                        last.then_inc(glu_ready, 1)
                        for j in range(2):
                            last = nc.scalar.activation(xl[:, e, j, :], ps_l[:, e % 2, j, :], ACT.Identity,
                                                        bias=B1l[:, e, j:j + 1], scale=-1.0)
                        last.then_inc(lin_ready, 1)
                    if a.live and e == 7:
                        a.wait(act, logit_gap)
                        a.free(act, routed, 1)
                        nc.scalar.activation(p1[:, :], df[:, :], ACT.Sigmoid).then_inc(shares, 1)
                        nc.scalar.activation(p2[:, :], df[:, :], ACT.Sigmoid, scale=-1.0).then_inc(shares, 1)
                    if b.live:
                        step(act, b, glu_ready, e)
                        step(act, b, act_ready, e, 4)
                        nc.scalar.activation(sg[:, e % 4, :, :], xg[:, e, :, :], ACT.Sigmoid,
                                             bias=s7[:, :], scale=-1.702).then_inc(gated, 1)
            pipeline(act, slot, units, LAG, U)

        @block.gpsimd
        def _(pool):
            nc.gpsimd.memset(halfneg[:, :], -0.5).then_inc(pool_n, 1)
            pool.wait_ge(pool_n, 1)

            def slot(at):
                a, b, d = (Tile(at, n_) for n_ in (0, 1, 2))
                for e in range(E):
                    if a.live and e == 1:
                        a.wait(pool, mean_sq)
                        a.free(pool, normed, 2)
                        nc.gpsimd.tensor_tensor(rr[:, a.u2, :], ms[:, :], halfneg[:, :], ALU.pow).then_inc(inv_rms, 1)
                    if d.live and e == 6:
                        d.wait(pool, ln_var)
                        d.free(pool, out_done, 2)
                        nc.gpsimd.tensor_tensor(rs[:, d.u2, :], ve[:, d.u2, :], halfneg[:, :],
                                                ALU.pow).then_inc(ln_rstd, 1)
                    o, oe = (b, e - 1) if e >= 1 else (d, 7)
                    if o.live:
                        step(pool, o, gated, oe)
                        step(pool, o, down, oe, E)
                        step(pool, o, prod_ready, oe)
                        nc.gpsimd.tensor_tensor(h[:, oe, :, :], pr[:, oe % 4, :, :], sg[:, oe % 4, :, :],
                                                ALU.mult).then_inc(act_ready, 1)
            pipeline(pool, slot, units, LAG, U)

        @block.vector
        def _(dve):
            n = Count(dve, dve_n)
            V = nc.vector
            dve.wait_ge(later.loaded, later.all_loaded)
            V.memset(s7[:, :], 7.0 * 1.702).then_inc(made, 1)
            V.tensor_scalar(B1g[:, :, :], B1[:, :, 0, :], -1.0, 7.0, ALU.mult, ALU.add).then_inc(made, 1)
            V.tensor_scalar(B1l[:, :, :], B1[:, :, 1, :], -1.0, -1.0, ALU.mult, ALU.add).then_inc(made, 1)

            def slot(at):
                a, b, c = (Tile(at, m) for m in (0, 1, 2))
                d = c

                def route(e, step_):
                    bc = lambda v: v.unsqueeze(2).to_broadcast([P, K, E])
                    rb = rt[:, :].unsqueeze(1).to_broadcast([P, K, E])
                    at_ = (e, step_)
                    if at_ == (0, 0):
                        a.wait(dve, squared)
                        a.free(dve, inv_rms, 1)
                        V.tensor_scalar(ms[:, :], ss[:, a.u2, :], 1.0 / P, 1e-5, ALU.mult, ALU.add).then_inc(mean_sq, 1)
                    if at_ == (2, 0):
                        a.wait(dve, inv_rms)
                        a.free(dve, t_turned, 1)
                        for k in range(K):
                            last = V.tensor_scalar(t[:, k, :], x[:, a.u2, k, :], rr[:, a.u2, k:k + 1], None, ALU.mult)
                        last.then_inc(normed, 1)
                    if at_ == (5, 0):
                        a.wait(dve, logits)
                        n.add(V.tensor_tensor(lg[:, :, :], ps_lg, gb[:, :].unsqueeze(1).to_broadcast([P, K, E]),
                                              ALU.add))
                    if at_ == (5, 1):
                        n.settle()
                        n.add(V.tensor_reduce(m1[:, :], lg[:, :, :], AX.X, ALU.max))
                    if at_ == (5, 2):
                        n.settle()
                        for k in range(K):
                            n.add(V.scalar_tensor_tensor(eq[:, k, :], lg[:, k, :], m1[:, k:k + 1], rt[:, :],
                                                         ALU.is_equal, ALU.mult))
                    if at_ == (6, 0):
                        n.settle()
                        n.add(V.tensor_reduce(r1[:, :], eq[:, :, :], AX.X, ALU.max))
                    if at_ == (6, 1):
                        n.settle()
                        n.add(V.tensor_tensor(oh1[:, :, :], rb, bc(r1[:, :]), ALU.is_equal))
                        n.settle()
                        n.add(V.scalar_tensor_tensor(l2[:, :, :], oh1[:, :, :], -3.0e38, lg[:, :, :], ALU.mult, ALU.add))
                    if at_ == (6, 2):
                        n.settle()
                        n.add(V.tensor_reduce(m2[:, :], l2[:, :, :], AX.X, ALU.max))
                    if at_ == (7, 0):
                        n.settle()
                        V.tensor_tensor(df[:, :], m1[:, :], m2[:, :], ALU.subtract).then_inc(logit_gap, 1)
                        for k in range(K):
                            n.add(V.scalar_tensor_tensor(eq[:, k, :], l2[:, k, :], m2[:, k:k + 1], rt[:, :],
                                                         ALU.is_equal, ALU.mult))
                    if at_ == (7, 1):
                        n.settle()
                        n.add(V.tensor_reduce(r2[:, :], eq[:, :, :], AX.X, ALU.max))
                for e in range(E):
                    if a.live:
                        route(e, 0)
                    if b.live and e == 0:
                        b.wait(dve, shares, 2)
                        n.settle()
                        b.free(dve, w_turned, 2)
                        for k in range(K):
                            n.add(V.tensor_scalar(oh1[:, k, :], rt[:, :], r1[:, k:k + 1], p1[:, k:k + 1],
                                                  ALU.is_equal, ALU.mult))
                            n.add(V.tensor_scalar(oh2[:, k, :], rt[:, :], r2[:, k:k + 1], p2[:, k:k + 1],
                                                  ALU.is_equal, ALU.mult))
                    o, oe = (b, e - 5) if e >= 5 else (c, e + 3)
                    if o.live:
                        step(dve, o, down, oe)
                        if oe == 0:
                            o.wait(dve, acc_ready)
                        else:
                            step(dve, o, added, oe, 1)
                        for k in range(K):
                            last = V.scalar_tensor_tensor(acc[:, o.u2, k, :], ps_y[:, oe % 2, k, :],
                                                          we[:, o.u2, k, oe:oe + 1], acc[:, o.u2, k, :],
                                                          ALU.mult, ALU.add)
                        last.then_inc(added, 1)
                    o, oe = (b, e - 1) if e >= 1 else (c, E - 1)
                    if o.live:
                        step(dve, o, clipped, oe)
                        step(dve, o, glu_ready, oe)
                        step(dve, o, act_ready, oe, 4)
                        V.scalar_tensor_tensor(pr[:, oe % 4, :, :], xg[:, oe, :, :], 7.0, xl[:, oe, :, :],
                                               ALU.subtract, ALU.mult).then_inc(prod_ready, 1)
                    if b.live:
                        step(dve, b, lin_ready, e)
                        V.tensor_scalar(xl[:, e, :, :], xl[:, e, :, :], -8.0, 6.0, ALU.max,
                                        ALU.min).then_inc(clipped, 1)
                    if a.live:
                        route(e, 1)
                    if b.live and e == 0:
                        n.settle()
                        V.tensor_tensor(we[:, b.u2, :, :], oh1[:, :, :], oh2[:, :, :], ALU.add).then_inc(routed, 1)
                    if b.live and e == 2:
                        b.wait(dve, w_turned)
                        V.tensor_copy(wT[:, :, :], ps_wT).then_inc(wT_ready, 1)
                    if b.live and e == 3:
                        b.wait(dve, biased)
                        b.free(dve, out_done, 2)
                        V.scalar_tensor_tensor(acc[:, b.u2, :, :], x[:, b.u2, :, :], 2.0, ps_b, ALU.mult,
                                               ALU.add).then_inc(acc_ready, 1)
                    if a.live and e == 5:
                        a.wait(dve, tT_ready)
                        a.free(dve, tT_split, 1, 2)
                        n.add(V.tensor_scalar(tTc[:, :].bitcast(U32), tT[:, a.u2, :].bitcast(U32), HIGH, None,
                                              ALU.bitwise_and))
                    if a.live and e == 6:
                        n.settle()
                        a.free(dve, up, 2, E)
                        V.tensor_copy(tTh[:, a.u2, :], tTc[:, :]).then_inc(tT_split, 1)
                        V.tensor_tensor(tTl[:, a.u2, :], tT[:, a.u2, :], tTc[:, :],
                                        ALU.subtract).then_inc(tT_split, 1)
                    if a.live:
                        route(e, 2)
                    if c.live and e == 4:
                        step(dve, c, added, E - 1)
                        for k in range(K):
                            n.add(V.bn_stats(st[:, k, :], acc[:, c.u2, k, :]))
                    if c.live and e == 5:
                        n.settle()
                        carry(dve, dve_passed)
                        for k in range(K):
                            n.add(V.bn_aggr(mv[:, c.u2, k, :], st[:, k, :]))
                    if c.live and e == 6:
                        n.settle()
                        V.tensor_scalar(ve[:, c.u2, :], mv[:, c.u2, :, 1], 1e-5, None, ALU.add).then_inc(ln_var, 1)
                    if c.live and e == 7:
                        c.wait(dve, ln_rstd)
                        c.wait_ring(dve, stored, 16, back=2)
                        for k in range(K):
                            last = V.tensor_scalar(xo[:, c.u2, k, :], acc[:, c.u2, k, :], mv[:, c.u2, k, 0:1],
                                                   rs[:, c.u2, k:k + 1], ALU.subtract, ALU.mult)
                        last.then_inc(out_done, 1)
            pipeline(dve, slot, units, LAG, U, [n])


def build(nc, ap, out):
    rows = ap["x"].shape[0]
    tiles = rows // P

    def scratch(name, width):
        return nc.dram_tensor(name, (rows, width), F32, kind="Internal").ap()

    v_dram, x1, x2 = scratch("v_dram", T), scratch("x1_dram", P), scratch("x2_dram", P)
    with ExitStack() as ctx:
        later = Later(nc, ctx, ap)
        attention(nc, *(ap[k] for k in ("x", "xT", "table", "table64", "table32")), v_dram, x1, tiles, later)
        cross_attention(nc, x1, ap["ctxT"], x2, tiles, later)
        experts(nc, x2, out, tiles, later)


def rope_tables():
    half = 16
    inv = (np.float32(1.0) / np.float32(10000.0) ** (np.arange(half, dtype=np.float32) * np.float32(2.0) / np.float32(32))).astype(np.float32)
    ang = np.arange(T, dtype=np.float32)[:, None] * inv[None, :]
    c, s = np.cos(ang).astype(np.float32), np.sin(ang).astype(np.float32)
    return np.tile(np.concatenate([c, c], 1), (2, 1)), np.tile(np.concatenate([-s, s], 1), (2, 1))


def mask_table():
    q = np.arange(P)[:, None] % T
    k = np.arange(T)[None, :]
    keys = np.where(k <= q, 0.0, NEG)
    blocks = np.where((np.arange(2)[None, :] + 1) * 32 - 1 <= q, 0.0, NEG)
    one = np.concatenate([keys, blocks, np.zeros((P, 3))], 1)
    return np.tile(one, (1, 4)).astype(np.float32)


def head_mask_table():
    return (np.arange(P)[:, None] // 8 % 4 == np.arange(4)[None, :]).astype(np.float32)


def rank_table():
    return np.broadcast_to(8.0 - np.arange(8), (P, 8)).astype(np.float32)


_OUT = (64, 64, 128)


def kernel(**inputs):
    import concourse.bacc as bacc
    from concourse.bass_utils import run_bass_kernel_spmd

    g = {k: np.asarray(v) for k, v in inputs.items()}
    x = g["x"].reshape(-1, P)
    a, xa, f = (lambda k, p=p: g["L0_" + p + k] for p in ("attn_", "xattn_", "ffn_"))
    rows = lambda v: np.broadcast_to(v, (P, v.shape[-1]))
    twice = lambda v: np.concatenate([v, v], 0)
    cos, sin = rope_tables()
    ident = np.eye(P, dtype=np.float32)
    arrays = {
        "x": x, "xT": x.T, "ctxT": g["ctx_1024"].reshape(-1, P).T,
        "table": np.concatenate([
            a("w_k"), a("w_v"), rows(a("g_qnorm")), rows(a("g_knorm")), twice(a("g_qnorm")[:, None]), twice(a("w_gate")),
            rows(a("b_gate")), rows(a("sink_logit")), cos, sin, mask_table(), ident], 1),
        "table64": np.concatenate([
            *a("w_out_group").transpose(0, 2, 1), *a("w_out").reshape(2, T, P)], 1),
        "table32": np.concatenate([a("w_qc").T, a("w_qup")], 1),
        "later_table": np.concatenate([
            ident, xa("Wq"), xa("Wk"), xa("Wv"), xa("Wo"), head_mask_table(), xa("bq")[:, None], xa("bk")[:, None],
            xa("bv")[:, None], f("norm_scale")[:, None], f("gate_w"), rows(f("gate_b")), rank_table(),
            f("mlp1_b").reshape(8, 2, P, 2).transpose(2, 0, 3, 1).reshape(P, -1),
            f("mlp2_w").reshape(8, 2, P, P).transpose(2, 0, 1, 3).reshape(P, -1)], 1),
        "bo": xa("bo"), "w1": f("mlp1_w").reshape(8, P, 256, 2).transpose(1, 0, 3, 2), "b2": f("mlp2_b"),
    }
    arrays = {k: np.ascontiguousarray(v) for k, v in arrays.items()}
    nc = bacc.Bacc("TRN2", target_bir_lowering=False, num_devices=1)
    ap = {k: nc.dram_tensor(f"in_{k}", v.shape, mybir.dt.from_np(v.dtype), kind="ExternalInput").ap()
          for k, v in arrays.items()}
    out = nc.dram_tensor("out_x", (x.shape[0], P), F32, kind="ExternalOutput").ap()
    build(nc, ap, out)
    r = run_bass_kernel_spmd(nc, [{f"in_{k}": v for k, v in arrays.items()}], core_ids=[0])
    return r.results[0]["out_x"].reshape(_OUT)
```
